# Optimizing a Trainium2 kernel written in Bass

```python
import numpy as np
import jax
import jax.numpy as jnp

def _softmax(x, axis=-1):
    return jax.nn.softmax(x, axis=axis)

def _gelu(x):
    return jax.nn.gelu(x, approximate=True)

def _silu(x):
    return jax.nn.silu(x)

def _sigmoid(x):
    return jax.nn.sigmoid(x)

def _layernorm(x, axis=-1, eps=1e-05):
    m = jnp.mean(x, axis=axis, keepdims=True)
    v = jnp.var(x, axis=axis, keepdims=True)
    return (x - m) / jnp.sqrt(v + eps)

def _scatter_add(tgt, idx, src, axis=0):
    return tgt.at[idx].add(src)

def _segment_sum(src, seg, n):
    return jax.ops.segment_sum(src, seg, n)
kernel_name = 'mk_flamingo_gated_d2_seqx_r8_bc422d'

def setup_inputs(seed: int=0):
    np.random.seed(seed)
    _w = jnp.asarray

    def _rec_inputs():
        import jax
        import jax.numpy as jnp
        _rk = jax.random.key(seed)
        x = 7.22e-05 + 1 * jax.random.normal(jax.random.fold_in(_rk, 1), (16, 56, 128), jnp.float32)
        _lenS = 56 - jax.random.randint(jax.random.fold_in(_rk, 7), (16,), 0, max(1, 56 // 4) + 1, jnp.int32)
        _lenS2 = 1500 - jax.random.randint(jax.random.fold_in(_rk, 8), (16,), 0, max(1, 1500 // 4) + 1, jnp.int32)
        _ctx_1024P = jax.random.normal(jax.random.fold_in(_rk, 11), (16, 16, 128), jnp.float32)
        _ctx_1024c = jax.random.dirichlet(jax.random.fold_in(_rk, 511), 0.3 * jnp.ones((16,), jnp.float32), (16, 1500))
        _ctx_1024t = jnp.einsum('bsk,bkd->bsd', _ctx_1024c, _ctx_1024P)
        _ctx_1024t = _ctx_1024t * jax.lax.rsqrt(jnp.mean(jnp.square(_ctx_1024t)) + 1e-12) * 0.953939
        ctx_1024 = 4.13588e-05 + 0.999923 * (_ctx_1024t + 0.3 * jax.random.normal(jax.random.fold_in(_rk, 611), (16, 1500, 128), jnp.float32))
        _validS = jnp.arange(56)[None, :] < _lenS[:, None]
        _validS2 = jnp.arange(1500)[None, :] < _lenS2[:, None]
        _causal = jnp.tril(jnp.ones((56, 56), dtype=bool))
        mask_BxSxS2_ik1 = jnp.where(jnp.broadcast_to(_validS2[:, None, :], (16, 56, 1500)), 1, 0).astype(jnp.int32)
        _g = jax.random.normal(jax.random.fold_in(_rk, 9001), (2, 2), jnp.float32)
        _g = jnp.sign(_g) * jnp.maximum(jnp.abs(_g), 1.0) + (_g == 0) * 1.0
        g_xattn = _g[0]
        g_ffn = _g[1]
        return (x, ctx_1024, mask_BxSxS2_ik1, g_xattn, g_ffn)
    x, ctx_1024, mask_BxSxS2_ik1, g_xattn, g_ffn = _rec_inputs()

    def _L0_xattn_setup():
        import jax, jax.numpy as jnp
        import numpy as np
        D_MODEL = 128
        NUM_HEADS = 16
        HEAD_DIM = D_MODEL // NUM_HEADS
        B, S = (4, 256)
        key = jax.random.key(seed)
        ks = jax.random.split(key, 11)
        scale = 1.0 / np.sqrt(D_MODEL)
        return {'query': jax.random.normal(ks[0], (B, S, D_MODEL), jnp.float32), 'key': jax.random.normal(ks[1], (B, S, D_MODEL), jnp.float32), 'value': jax.random.normal(ks[2], (B, S, D_MODEL), jnp.float32), 'Wq': jax.random.normal(ks[3], (D_MODEL, D_MODEL), jnp.float32) * scale, 'bq': jnp.zeros((D_MODEL,), jnp.float32), 'Wk': jax.random.normal(ks[4], (D_MODEL, D_MODEL), jnp.float32) * scale, 'bk': jnp.zeros((D_MODEL,), jnp.float32), 'Wv': jax.random.normal(ks[5], (D_MODEL, D_MODEL), jnp.float32) * scale, 'bv': jnp.zeros((D_MODEL,), jnp.float32), 'Wo': jax.random.normal(ks[6], (D_MODEL, D_MODEL), jnp.float32) * scale, 'bo': jnp.zeros((D_MODEL,), jnp.float32)}
    _L0_xattn_all = _L0_xattn_setup()
    _L0_xattn_in = {k: v for k, v in _L0_xattn_all.items() if k in ('Wq', 'bq', 'Wk', 'bk', 'Wv', 'bv', 'Wo', 'bo')}
    del _L0_xattn_all

    def _L0_ffn_setup():
        import jax, jax.numpy as jnp
        import numpy as np
        TOP_K = 2
        key = jax.random.key(seed)
        ks = jax.random.split(key, 6)
        B, S, D, F, E = (2, 256, 128, 512, 8)
        sd = 1.0 / np.sqrt(D)
        sf = 1.0 / np.sqrt(F)
        return {'x': jax.random.normal(ks[0], (B, S, D), jnp.float32), 'gate_w': jax.random.normal(ks[1], (D, E), jnp.float32) * sd, 'w1': jax.random.normal(ks[2], (E, D, F), jnp.float32) * sd, 'b1': jax.random.normal(ks[3], (E, F), jnp.float32) * 0.01, 'w2': jax.random.normal(ks[4], (E, F, D), jnp.float32) * sf, 'b2': jax.random.normal(ks[5], (E, D), jnp.float32) * 0.01}
    _L0_ffn_all = _L0_ffn_setup()
    _L0_ffn_in = {k: v for k, v in _L0_ffn_all.items() if k in ('gate_w', 'w1', 'b1', 'w2', 'b2')}
    del _L0_ffn_all

    def _L1_xattn_setup():
        import jax, jax.numpy as jnp
        import numpy as np
        B, S, D, H = (2, 256, 128, 16)
        HD = D // H
        key = jax.random.key(seed)
        ks = jax.random.split(key, 12)
        s = 1.0 / np.sqrt(D)
        return {'query': jax.random.normal(ks[0], (B, S, D), jnp.float32), 'key': jax.random.normal(ks[1], (B, S, D), jnp.float32), 'value': jax.random.normal(ks[2], (B, S, D), jnp.float32), 'mask': jax.random.randint(ks[3], (B, S, S), 0, 2, jnp.int32), 'wq_kernel': jax.random.normal(ks[4], (D, D), jnp.float32) * s, 'wq_bias': jnp.zeros((D,), jnp.float32), 'wk_kernel': jax.random.normal(ks[5], (D, D), jnp.float32) * s, 'wk_bias': jnp.zeros((D,), jnp.float32), 'wv_kernel': jax.random.normal(ks[6], (D, D), jnp.float32) * s, 'wv_bias': jnp.zeros((D,), jnp.float32), 'wo_kernel': jax.random.normal(ks[7], (D, D), jnp.float32) * s, 'wo_bias': jnp.zeros((D,), jnp.float32)}
    _L1_xattn_all = _L1_xattn_setup()
    _L1_xattn_in = {k: v for k, v in _L1_xattn_all.items() if k in ('wq_kernel', 'wq_bias', 'wk_kernel', 'wk_bias', 'wv_kernel', 'wv_bias', 'wo_kernel', 'wo_bias')}
    del _L1_xattn_all

    def _L1_ffn_setup():
        import jax, jax.numpy as jnp
        import numpy as np
        B, S, D, E, H, K = (4, 256, 128, 8, 64, 2)
        key = jax.random.key(seed)
        ks = jax.random.split(key, 11)
        sc = 0.02
        return {'x': jax.random.normal(ks[0], (B, S, D), dtype=jnp.float32), 'gate_W': jax.random.normal(ks[1], (D, E), dtype=jnp.float32) * sc, 'W1': jax.random.normal(ks[2], (E, D, H), dtype=jnp.float32) * sc, 'b1': jnp.zeros((E, H), dtype=jnp.float32), 'W2': jax.random.normal(ks[3], (E, H, D), dtype=jnp.float32) * sc, 'b2': jnp.zeros((E, D), dtype=jnp.float32), 'Ws1': jax.random.normal(ks[4], (D, H), dtype=jnp.float32) * sc, 'bs1': jnp.zeros((H,), dtype=jnp.float32), 'Ws2': jax.random.normal(ks[5], (H, D), dtype=jnp.float32) * sc, 'bs2': jnp.zeros((D,), dtype=jnp.float32), 'route_scale': jnp.ones((), dtype=jnp.float32)}
    _L1_ffn_all = _L1_ffn_setup()
    _L1_ffn_in = {k: v for k, v in _L1_ffn_all.items() if k in ('gate_W', 'W1', 'b1', 'W2', 'b2', 'Ws1', 'bs1', 'Ws2', 'bs2', 'route_scale')}
    del _L1_ffn_all
    return {'x': x, 'ctx_1024': ctx_1024, 'mask_BxSxS2_ik1': mask_BxSxS2_ik1, 'g_xattn': g_xattn, 'g_ffn': g_ffn, 'L0_xattn_Wq': _L0_xattn_in['Wq'], 'L0_xattn_bq': _L0_xattn_in['bq'], 'L0_xattn_Wk': _L0_xattn_in['Wk'], 'L0_xattn_bk': _L0_xattn_in['bk'], 'L0_xattn_Wv': _L0_xattn_in['Wv'], 'L0_xattn_bv': _L0_xattn_in['bv'], 'L0_xattn_Wo': _L0_xattn_in['Wo'], 'L0_xattn_bo': _L0_xattn_in['bo'], 'L0_ffn_gate_w': _L0_ffn_in['gate_w'], 'L0_ffn_w1': _L0_ffn_in['w1'], 'L0_ffn_b1': _L0_ffn_in['b1'], 'L0_ffn_w2': _L0_ffn_in['w2'], 'L0_ffn_b2': _L0_ffn_in['b2'], 'L1_xattn_wq_kernel': _L1_xattn_in['wq_kernel'], 'L1_xattn_wq_bias': _L1_xattn_in['wq_bias'], 'L1_xattn_wk_kernel': _L1_xattn_in['wk_kernel'], 'L1_xattn_wk_bias': _L1_xattn_in['wk_bias'], 'L1_xattn_wv_kernel': _L1_xattn_in['wv_kernel'], 'L1_xattn_wv_bias': _L1_xattn_in['wv_bias'], 'L1_xattn_wo_kernel': _L1_xattn_in['wo_kernel'], 'L1_xattn_wo_bias': _L1_xattn_in['wo_bias'], 'L1_ffn_gate_W': _L1_ffn_in['gate_W'], 'L1_ffn_W1': _L1_ffn_in['W1'], 'L1_ffn_b1': _L1_ffn_in['b1'], 'L1_ffn_W2': _L1_ffn_in['W2'], 'L1_ffn_b2': _L1_ffn_in['b2'], 'L1_ffn_Ws1': _L1_ffn_in['Ws1'], 'L1_ffn_bs1': _L1_ffn_in['bs1'], 'L1_ffn_Ws2': _L1_ffn_in['Ws2'], 'L1_ffn_bs2': _L1_ffn_in['bs2'], 'L1_ffn_route_scale': _L1_ffn_in['route_scale']}

def reference(x, ctx_1024, mask_BxSxS2_ik1, g_xattn, g_ffn, L0_xattn_Wq, L0_xattn_bq, L0_xattn_Wk, L0_xattn_bk, L0_xattn_Wv, L0_xattn_bv, L0_xattn_Wo, L0_xattn_bo, L0_ffn_gate_w, L0_ffn_w1, L0_ffn_b1, L0_ffn_w2, L0_ffn_b2, L1_xattn_wq_kernel, L1_xattn_wq_bias, L1_xattn_wk_kernel, L1_xattn_wk_bias, L1_xattn_wv_kernel, L1_xattn_wv_bias, L1_xattn_wo_kernel, L1_xattn_wo_bias, L1_ffn_gate_W, L1_ffn_W1, L1_ffn_b1, L1_ffn_W2, L1_ffn_b2, L1_ffn_Ws1, L1_ffn_bs1, L1_ffn_Ws2, L1_ffn_bs2, L1_ffn_route_scale):
    import jax
    import jax.numpy as jnp

    def _L0_xattn_ref(query, key, value, Wq, bq, Wk, bk, Wv, bv, Wo, bo):
        import jax, jax.numpy as jnp
        import numpy as np
        D_MODEL = 128
        NUM_HEADS = 16
        HEAD_DIM = D_MODEL // NUM_HEADS
        B, S = (4, 256)
        b = query.shape[0]

        def split_heads(x):
            return x.reshape(b, -1, NUM_HEADS, HEAD_DIM).transpose(0, 2, 1, 3)
        q = split_heads(query @ Wq.T + bq)
        k = split_heads(key @ Wk.T + bk)
        v = split_heads(value @ Wv.T + bv)
        scores = jnp.einsum('bhqd,bhkd->bhqk', q, k) / np.sqrt(HEAD_DIM)
        weights = jax.nn.softmax(scores, axis=-1)
        out = jnp.einsum('bhqk,bhkd->bhqd', weights, v)
        out = out.transpose(0, 2, 1, 3).reshape(b, -1, D_MODEL)
        return out @ Wo.T + bo

    def _L0_ffn_ref(x, gate_w, w1, b1, w2, b2):
        import jax, jax.numpy as jnp
        import numpy as np
        TOP_K = 2
        B, S, D = x.shape
        T = B * S
        xf = x.reshape(T, D)
        gate_scores = jax.nn.softmax(xf @ gate_w, axis=-1)
        topk_scores, topk_idx = jax.lax.top_k(gate_scores, TOP_K)
        topk_scores = topk_scores / jnp.sum(topk_scores, axis=-1, keepdims=True)
        h = jax.nn.gelu(jnp.einsum('td,edf->etf', xf, w1) + b1[:, None, :], approximate=False)
        y = jnp.einsum('etf,efd->etd', h, w2) + b2[:, None, :]
        tok = jnp.arange(T)
        y_sel = y[topk_idx.T, tok[None, :]]
        out = jnp.einsum('kt,ktd->td', topk_scores.T, y_sel)
        return out.reshape(B, S, D)

    def _L1_xattn_ref(query, key, value, mask, wq_kernel, wq_bias, wk_kernel, wk_bias, wv_kernel, wv_bias, wo_kernel, wo_bias):
        import jax, jax.numpy as jnp
        import numpy as np
        B, S, D, H = (2, 256, 128, 16)
        HD = D // H
        b = query.shape[0]

        def split_heads(x):
            return x.reshape(b, -1, H, HD).transpose(0, 2, 1, 3)
        q = split_heads(query @ wq_kernel + wq_bias)
        k = split_heads(key @ wk_kernel + wk_bias)
        v = split_heads(value @ wv_kernel + wv_bias)
        scores = jnp.einsum('bhqd,bhkd->bhqk', q, k) / jnp.sqrt(jnp.float32(HD))
        m = mask[:, None, :, :]
        scores = jnp.where(m == 0, jnp.float32(-1000000000.0), scores)
        attn = jax.nn.softmax(scores, axis=-1)
        out = jnp.einsum('bhqk,bhkd->bhqd', attn, v)
        out = out.transpose(0, 2, 1, 3).reshape(b, -1, D)
        return out @ wo_kernel + wo_bias

    def _L1_ffn_ref(x, gate_W, W1, b1, W2, b2, Ws1, bs1, Ws2, bs2, route_scale):
        import jax, jax.numpy as jnp
        import numpy as np
        B, S, D, E, H, K = (4, 256, 128, 8, 64, 2)
        scores = jax.nn.sigmoid(x @ gate_W) * route_scale
        topk_scores, topk_idx = jax.lax.top_k(scores, K)
        topk_w = topk_scores / topk_scores.sum(-1, keepdims=True)
        onehot = jax.nn.one_hot(topk_idx, E, dtype=x.dtype)
        gate_full = jnp.einsum('bsk,bske->bse', topk_w, onehot)
        h = jax.nn.gelu(jnp.einsum('bsd,edh->bseh', x, W1) + b1, approximate=False)
        y = jnp.einsum('bseh,ehd->bsed', h, W2) + b2
        expert_out = jnp.einsum('bse,bsed->bsd', gate_full, y)
        shared = jax.nn.gelu(x @ Ws1 + bs1, approximate=False) @ Ws2 + bs2
        return expert_out + shared
    x = x + jnp.tanh(g_xattn[0]) * _L0_xattn_ref(_layernorm(x, axis=-1), ctx_1024, ctx_1024, L0_xattn_Wq, L0_xattn_bq, L0_xattn_Wk, L0_xattn_bk, L0_xattn_Wv, L0_xattn_bv, L0_xattn_Wo, L0_xattn_bo)
    x = x + jnp.tanh(g_ffn[0]) * _L0_ffn_ref(_layernorm(x, axis=-1), L0_ffn_gate_w, L0_ffn_w1, L0_ffn_b1, L0_ffn_w2, L0_ffn_b2)
    x = x + jnp.tanh(g_xattn[1]) * _L1_xattn_ref(_layernorm(x, axis=-1), ctx_1024, ctx_1024, mask_BxSxS2_ik1, L1_xattn_wq_kernel, L1_xattn_wq_bias, L1_xattn_wk_kernel, L1_xattn_wk_bias, L1_xattn_wv_kernel, L1_xattn_wv_bias, L1_xattn_wo_kernel, L1_xattn_wo_bias)
    x = x + jnp.tanh(g_ffn[1]) * _L1_ffn_ref(_layernorm(x, axis=-1), L1_ffn_gate_W, L1_ffn_W1, L1_ffn_b1, L1_ffn_W2, L1_ffn_b2, L1_ffn_Ws1, L1_ffn_bs1, L1_ffn_Ws2, L1_ffn_bs2, L1_ffn_route_scale)
    return x

_drawn_inputs = setup_inputs


def setup_inputs(seed=0):
    import zlib

    import numpy as np

    out = dict(_drawn_inputs(seed))
    spreads = {'g_ffn': (-1.0, 0.6),
     'L0_xattn_bq': (0.0, 0.1),
     'L0_xattn_bk': (0.0, 0.8),
     'L0_xattn_bv': (0.0, 0.1),
     'L0_xattn_bo': (0.0, 0.1),
     'L1_xattn_wq_bias': (0.0, 0.462),
     'L1_xattn_wk_bias': (0.0, 0.8),
     'L1_xattn_wv_bias': (0.0, 0.1),
     'L1_xattn_wo_bias': (0.0, 0.1),
     'L1_ffn_b1': (0.0, 0.8),
     'L1_ffn_b2': (0.0, 0.1),
     'L1_ffn_bs1': (0.0, 0.8),
     'L1_ffn_bs2': (0.0, 0.1)}
    factors = {'L0_ffn_b1': 8.0,
     'L0_ffn_b2': 8.0,
     'L1_ffn_W1': 6.591,
     'L1_ffn_W2': 6.009,
     'L1_ffn_Ws1': 4.639,
     'L1_ffn_Ws2': 4.33}
    for name, (base, spread) in spreads.items():
        noise = np.random.default_rng([zlib.crc32(name.encode()), seed]).standard_normal(out[name].shape)
        drawn = base * np.exp(spread * noise) if base else spread * noise
        out[name] = jnp.asarray(drawn.astype(out[name].dtype))
    for name, factor in factors.items():
        out[name] = (out[name] * factor).astype(out[name].dtype)
    return out
```

```python
from contextlib import ExitStack

import concourse.bass as bass
from concourse import mybir

ALU = mybir.AluOpType
ACT = mybir.ActivationFunctionType
AX = mybir.AxisListType
F32 = mybir.dt.float32
F16 = mybir.dt.float16
I32 = mybir.dt.int32

LAYERS = 2
B, S, D, S2 = 16, 56, 128, 1500
H = 16
HD = D // H
PAIRS = H // 2
PR = 2 * HD
G = B // 2
T = 2 * S
NB = LAYERS * B
KT, KP = 12, 125
CH, CW = 3, 500
KPC = CW // KP
MASK0 = 3 * PR
SHIFT0 = MASK0 + S
ROWS = SHIFT0 + 2
RING = 4
NMAX = CH * PAIRS
MAXES_PER_KT = 3
QK_SCALE = 4.0
EXP_SCALE = 1.0 / (QK_SCALE * QK_SCALE * float(HD) ** 0.5)
BIG = 32768.0
EPS = 1e-5
E0, F0C = 8, 4
E1, F1 = 8, 64
NE = 8

COLS = {}
_at = 0
for _name, _n in (("wq0", D), ("wk0", D), ("wv0", D), ("wq1", D), ("wk1", D), ("wv1", D),
                  ("bk0", 1), ("bk1", 1), ("gate0", NE), ("gate1", NE), ("b1_0", E0 * F0C),
                  ("b1_1", E1 * F1 // 128), ("ws1", F1)):
    COLS[_name] = (_at, _at + _n)
    _at += _n
NCOLS = _at
BO, GX, GF, RS, NBC = 0, 2 * D, 2 * D + 2, 2 * D + 4, 2 * D + 5


def has_k(s):
    return -1 <= s <= NB - 2


def has_v(s):
    return 0 <= s <= NB - 1


def has_m(s):
    return 0 <= s <= NB - 1


def has_e(s):
    return 1 <= s <= NB


def has_tail(s):
    return 2 <= s <= NB + 1


def has_q(s):
    return s % 2 == 1 and -1 <= s <= NB - 3


def has_a(s):
    return s % 2 == 1 and 3 <= s <= NB + 1


def has_f(s):
    return s % 2 == 0 and 4 <= s <= NB + 2


def layer_of(n):
    return n // B


def kv_uses(s):
    uses = []
    for c in range(CH):
        if has_k(s):
            uses.append((2 * c + 1, f"k{c}", 1))
        if has_v(s):
            uses.append((2 * c + 2, f"v{c}", 1))
    return uses


def fh_uses(s):
    uses = []
    if has_q(s):
        uses += [(5, "qT", 2), (6, "q", 1)]
    if has_a(s):
        if layer_of(s - 2) == 0:
            uses += [(7 + e, f"h{e}", 1) for e in range(5)]
        else:
            uses += [(7, "h0", 1), (8, "h1", 1)]
    if has_f(s) and layer_of(s - 3) == 0:
        uses += [(e - 5, f"h{e}", 1) for e in range(5, 8)]
    return uses


def fy_uses(s):
    uses = []
    if has_a(s):
        uses += [(2, "sum", 1), (3, "y", 1), (5, "xT", 1), (6, "lg", 1), (10, "gT", 1)]
    if has_f(s):
        uses += [(4 + i, f"y{i}", 1) for i in range(4)] + [(8, "yb", 1)]
    if has_m(s):
        uses.append((9, "ct", 1))
    return sorted(uses)


def experts_of(i):
    e = 4 * (i // 2) + i % 2
    return e, e + 2


def before(uses, s, freed=False):
    return sum(u[2] if freed else 1 for t in range(-1, s) for u in uses(t))


def upto(uses, s, name, freed=False):
    n = before(uses, s, freed)
    for u in uses(s):
        n += u[2] if freed else 1
        if u[1] == name:
            return n
    raise KeyError((s, name))


def links(s):
    n = 0
    if has_m(s):
        n += 2
    if has_q(s):
        n += 2
    if has_a(s):
        n += 13
    if has_f(s):
        n += 4
    return n


def b_total(n):
    return 48 * min(n + 1, B) + 64 * max(0, n + 1 - B)


class Step:

    def __init__(self, s0, turn=None, turns=1):
        self.s, self.turn, self.turns = s0, turn, turns

    def at(self, f):
        v = f(self.s)
        if self.turn is None:
            return v
        d = f(self.s + 2) - v
        assert all(f(self.s + 2 * i) == v + i * d for i in range(self.turns))
        return v + self.turn * d if d else v


PEELED_AND_LOOPS = [-1, 0, 1, 2, (3, 5), 13, 14, 15, 16, 17, 18, (19, 5), 29, 30, 31, 32, 33, 34]


def run_steps(eng, step):
    for item in PEELED_AND_LOOPS:
        if isinstance(item, tuple):
            s0, turns = item
            with eng.Fori(0, turns) as turn:
                step(Step(s0, turn, turns))
                step(Step(s0 + 1, turn, turns))
        else:
            step(Step(item))


def build(nc, x, ctxT, mask, wpack, bqrow, bcast, wo, bvc, w1_0, w2_0, b2_0, w1_1, w2_1, b2_1, ws2, bs1, out):
    with ExitStack() as ctx:
        def sb(name, shape, dt=F32):
            return ctx.enter_context(nc.sbuf_tensor(name, shape, dt))

        def ps(name, shape):
            return ctx.enter_context(nc.psum_tensor(name, shape, F32))

        def sem(name):
            return ctx.enter_context(nc.semaphore(name))

        W = sb("W", [128, NCOLS])

        def w(name):
            a, b = COLS[name]
            return W[:, a:b]

        bq_row = sb("bq_row", [1, LAYERS * D])
        bc = sb("bc", [128, NBC])
        gains = sb("gains", [128, 4])
        tbo = sb("tbo", [T, LAYERS, D])
        woE = sb("woE", [128, LAYERS, 2, D])
        bvE = sb("bvE", [128, LAYERS, 2])
        w1a = sb("w1a", [128, E0, F0C * 128])
        w2a = sb("w2a", [128, E0, F0C, D])
        w1b = sb("w1b", [128, E1, F1])
        w2b = sb("w2b", [128, E1 // 2, D])
        ws2b = sb("ws2b", [F1, D])
        bs1b = sb("bs1b", [F1, 1])
        b2x = sb("b2x", [NE + 1, LAYERS, D])
        ident = sb("ident", [128, 128])
        ident16 = sb("ident16", [128, 128], F16)
        sel = sb("sel", [128, 128])
        rowmask = sb("rowmask", [128, 4])
        headmask = sb("headmask", [128, 2, 2, S])
        bvm = sb("bvm", [128, LAYERS, 2, 2, S])
        ones = sb("ones", [128, T])
        before_me = sb("before_me", [T, NE, NE])
        mhalf = sb("mhalf", [T, 1])
        pick = sb("pick", [S, H, S], F16)

        X = sb("X", [T, G * D])
        C = sb("C", [128, 2, S2])
        khi = sb("khi", [128, S2], F16)
        klo = sb("klo", [128, S2], F16)
        kop = sb("kop", [128, 2, PAIRS, S2], F16)
        qmax = sb("qmax", [128, 2, PAIRS, 2, S], F16)
        qexp = sb("qexp", [128, 2, PAIRS, 2, S], F16)
        V = sb("V", [128, 2, KT, PAIRS, 32])
        P = sb("P", [128, RING, PAIRS * T])
        maskin = sb("maskin", [T, S2], I32)
        maskop = sb("maskop", [T, S2], F16)
        shift_rows = maskin[0:1, :].bitcast(F16).rearrange("a (i n) -> a i n", i=2)
        masksink = sb("masksink", [T, S2], F16)
        masksum = sb("masksum", [T, 1])
        keep = sb("keep", [T, 1])
        stq, mvq = sb("stq", [T, 6]), sb("mvq", [T, 2])
        stf, mvf = sb("stf", [T, 6]), sb("mvf", [T, 2])
        veq, rsq, rkq = sb("veq", [T, 1]), sb("rsq", [T, 1]), sb("rkq", [T, 1])
        vef, rsf = sb("vef", [T, 1]), sb("rsf", [T, 1])
        xnq = sb("xnq", [T, D])
        xnqT = sb("xnqT", [128, T])
        keepT = sb("keepT", [1, T])
        qhi = sb("qhi", [128, T], F16)
        qlo = sb("qlo", [128, T], F16)
        mx = sb("mx", [T, 2, CH, PAIRS])
        m8 = sb("m8", [T, PAIRS])
        cc = sb("cc", [T, 2, PAIRS], F16)
        ct = sb("ct", [2 * PAIRS, T], F16)
        OM = sb("OM", [128, 2, 2 * T])
        rden = sb("rden", [128, 4 * T])
        ON0 = sb("ON0", [128, 4 * T])
        ON = sb("ON", [128, 2, 2, 2, S])
        XF0, XF = sb("XF0", [T, D]), sb("XF", [T, D])
        xnf = sb("xnf", [T, D])
        xnfT = sb("xnfT", [128, T])
        lg = sb("lg", [T, NE])
        lmax, lneg = sb("lmax", [T, 1]), sb("lneg", [T, 1])
        ge, gse = sb("ge", [T, NE]), sb("gse", [T, 1])
        g1, g2 = sb("g1", [T, NE]), sb("g2", [T, NE])
        gp = sb("gp", [T, NE])
        ggt, geq, gel, grk = (sb(n, [T, NE, NE]) for n in ("ggt", "geq", "gel", "grk"))
        rank, gsp = sb("rank", [T, NE]), sb("gsp", [T, NE])
        gden, grd = sb("gden", [T, 1]), sb("grd", [T, 1])
        gate = sb("gate", [T, NE + 1])
        gateT = sb("gateT", [NE + 1, T])
        HR = sb("HR", [128, E0 * F0C, T])
        acc = sb("acc", [T, 2, D])

        pMX = ps("pMX", [128, 2, 512])
        pST = ps("pST", [128, 2, 512])
        pO = ps("pO", [128, 512])
        pKV = ps("pKV", [128, 512])
        pFH = ps("pFH", [128, 512])
        pFY = ps("pFY", [128, 512])

        w_in, x_in, f_in, wo_in = sem("w_in"), sem("x_in"), sem("f_in"), sem("wo_in")
        c_in = [sem("c_in0"), sem("c_in1")]
        mask_in = sem("mask_in")
        init_p = sem("init_p")
        init_v = sem("init_v")
        init_w = sem("init_w")
        init_a = sem("init_a")
        init_dma = sem("init_dma")
        kop_in = [sem(f"kop_in{c}") for c in range(CH)]
        qmax_in = sem("qmax_in")
        qexp_in = [sem("qexp_in0"), sem("qexp_in1")]
        shift_in = sem("shift_in")
        mask_done, masksum_done, keep_done = sem("mask_done"), sem("masksum_done"), sem("keep_done")
        khi_done = sem("khi_done")
        kv_ready, kv_free = sem("kv_ready"), sem("kv_free")
        mx_ready, max_done = sem("mx_ready"), sem("max_done")
        cc_ready = sem("cc_ready")
        st_ready, exp_done = sem("st_ready"), sem("exp_done")
        av_done, o_free = sem("av_done"), sem("o_free")
        fh_ready, fh_free = sem("fh_ready"), sem("fh_free")
        fy_ready, fy_free = sem("fy_ready"), sem("fy_free")
        statq_done, rstdq_done, xnq_done = sem("statq_done"), sem("rstdq_done"), sem("xnq_done")
        statf_done, rstdf_done, xnf_done = sem("statf_done"), sem("rstdf_done"), sem("xnf_done")
        on_done = sem("on_done")
        logit_done, gexp_done, gate_done = sem("logit_done"), sem("gexp_done"), sem("gate_done")
        gelu_done = sem("gelu_done")
        x_done = sem("x_done")
        dve_link, pool_link = sem("dve_link"), sem("pool_link")
        stored = sem("stored")
        passed = sem("passed")

        block = ctx.enter_context(nc.Block())

        def apart(eng):
            eng.sem_inc(passed, 1)

        def groups(f):
            return lambda s: sum(f(t) for t in range(-1, s))

        q_count, a_count, f_count = groups(has_q), groups(has_a), groups(has_f)

        def mask_count(s):
            return sum(has_q(t) and t + 1 >= B for t in range(-1, s))

        @block.sync
        def _(sp):
            sp.dma_start(W[:, :], wpack).then_inc(w_in, 16)
            sp.dma_start(C[:, 0, :], ctxT[0]).then_inc(c_in[0], 16)
            sp.dma_start(X[:, :].rearrange("t (g d) -> t g d", g=G),
                         x.rearrange("(g t) d -> t g d", g=G)).then_inc(x_in, 16)
            sp.dma_start(bq_row[:, :], bqrow).then_inc(w_in, 16)
            sp.dma_start(bc[:, :], bcast.partition_broadcast(128)).then_inc(w_in, 16)
            sp.wait_ge(init_v, 2)
            sp.wait_ge(init_p, 5)
            for b in range(2):
                sp.dma_start(kop[MASK0:SHIFT0, b, :, :],
                             maskop[0:S, :].unsqueeze(1).broadcast_to([S, PAIRS, S2])).then_inc(init_dma, 16)
                for i in range(2):
                    sp.dma_start(kop[SHIFT0 + i:SHIFT0 + i + 1, b, :, :],
                                 shift_rows[:, i:i + 1, :].broadcast_to([1, PAIRS, S2])).then_inc(init_dma, 16)
                sp.dma_start(qmax[MASK0:SHIFT0, b, :, :, :],
                             pick[:, :, :].rearrange("s (p j) q -> s p j q", j=2)).then_inc(init_dma, 16)
            sp.dma_start(C[:, 1, :], ctxT[1]).then_inc(c_in[1], 16)
            sp.wait_ge(init_w, 3)
            for l in range(LAYERS):
                for g in range(4):
                    sp.dma_start(woE[32 * g:32 * g + PR, l, :, :],
                                 wo[l].rearrange("(r g i) n -> g i r n", r=2, g=4)[g]).then_inc(wo_in, 16)
                    sp.dma_start(bvE[32 * g:32 * g + PR, l, :], bvc[l, g]).then_inc(wo_in, 16)
            sp.dma_start(w1a[:, :, :], w1_0.rearrange("e d f -> d e f")).then_inc(f_in, 16)
            sp.dma_start(w2a[:, :, :, :], w2_0.rearrange("e (c f) d -> f e c d", c=F0C)).then_inc(f_in, 16)
            sp.dma_start(w1b[:, :, :], w1_1.rearrange("e d f -> d e f")).then_inc(f_in, 16)
            sp.dma_start(w2b[:, :, :], w2_1.rearrange("(c e) f d -> (e f) c d", e=2)).then_inc(f_in, 16)
            sp.dma_start(b2x[0:NE, 0, :], b2_0).then_inc(f_in, 16)
            sp.dma_start(b2x[:, 1, :], b2_1).then_inc(f_in, 16)
            sp.dma_start(ws2b[:, :], ws2).then_inc(f_in, 16)
            sp.dma_start(bs1b[:, :], bs1).then_inc(f_in, 16)
            sp.wait_ge(init_dma, 128)

            def key_chunk(st, c):
                s, cols = st.s, slice(c * CW, (c + 1) * CW)
                dst = (s + 1) % 2
                sp.wait_ge(kv_free, st.at(lambda s: upto(kv_uses, s, f"k{c}", True)))
                apart(sp)
                if has_e(s):
                    sp.wait_ge(st_ready, st.at(lambda s: 2 * (KT * (s - 1) + KPC * (c + 1))))
                    apart(sp)
                if s + 1 >= B and c == 0 and s % 2:
                    sp.wait_ge(mask_done, st.at(lambda s: mask_count(s) + 1))
                    apart(sp)
                for row, part in ((0, khi), (PR, klo), (2 * PR, khi)):
                    sp.dma_start(kop[row:row + PR, dst, :, cols], part[:, cols]).then_inc(kop_in[c], 16)
                if s + 1 >= B:
                    half = S * ((s + 1) % 2)
                    sp.dma_start(kop[MASK0:SHIFT0, dst, :, cols],
                                 maskop[half:half + S, cols].unsqueeze(1).broadcast_to([S, PAIRS, CW])
                                 ).then_inc(kop_in[c], 16)

            def step(st):
                s = st.s
                if has_m(s):
                    sp.wait_ge(qmax_in, st.at(lambda s: 96 * (s + 1)))
                    apart(sp)
                    if has_tail(s):
                        sp.wait_ge(st_ready, st.at(lambda s: 2 * KT * (s - 1)))
                        apart(sp)
                    sp.dma_start(qexp[0:SHIFT0, s % 2, :, :, :], qmax[0:SHIFT0, s % 2, :, :, :]).then_inc(qexp_in[s % 2], 16)
                if has_k(s):
                    key_chunk(st, 0)
                    if has_q(s):
                        sp.wait_ge(fh_free, st.at(lambda s: upto(fh_uses, s, "q", True)))
                        apart(sp)
                    if s >= 1:
                        sp.wait_ge(mx_ready, st.at(lambda s: NMAX * s))
                        apart(sp)
                        sp.wait_ge(qexp_in[(s - 1) % 2], st.at(lambda s: 16 * ((s - 1) // 2 + 1)))
                        apart(sp)
                    half = S * ((s + 1) % 2)
                    for row, part in ((0, qhi), (PR, qhi), (2 * PR, qlo)):
                        for j in range(2):
                            sp.dma_start(qmax[row + HD * j:row + HD * (j + 1), (s + 1) % 2, :, j, :],
                                         part[64 * j:64 * (j + 1), half:half + S]).then_inc(qmax_in, 16)
                if s % 2 == 0 and B - 2 <= s <= NB - 4:
                    group = st.at(lambda s: (s + 2 - B) // 2)
                    if s > B - 2:
                        sp.wait_ge(mask_done, st.at(mask_count))
                        apart(sp)
                    src = mask[group] if isinstance(group, int) else mask[bass.ds(group, 1)].rearrange("a t k -> (a t) k")
                    sp.dma_start(maskin[:, :], src).then_inc(mask_in, 16)
                if 0 <= s <= NB - 3:
                    batch = st.at(lambda s: (s + 2) % B)
                    sp.wait_ge(kv_ready, st.at(lambda s: upto(kv_uses, s, "v2")))
                    apart(sp)
                    src = ctxT[batch] if isinstance(batch, int) else ctxT[bass.ds(batch, 1)].rearrange("a d k -> (a d) k")
                    sp.dma_start(C[:, s % 2, :], src).then_inc(c_in[s % 2], 16)
                if has_k(s):
                    key_chunk(st, 1)
                if has_m(s):
                    sp.wait_ge(fy_free, st.at(lambda s: upto(fy_uses, s, "ct", True)))
                    apart(sp)
                    sp.dma_start(qexp[SHIFT0:ROWS, s % 2, :, :, :].rearrange("r p j q -> r (p j q)"),
                                 ct[:, :]).then_inc(shift_in, 16)
                if has_k(s):
                    key_chunk(st, 2)

            run_steps(sp, step)
            sp.wait_ge(x_done, 2 * G)
            sp.dma_start(out.rearrange("(g t) d -> t g d", g=G),
                         X[:, :].rearrange("t (g d) -> t g d", g=G)).then_inc(stored, 16)
            sp.wait_ge(stored, 16)

        @block.gpsimd
        def _(pool):
            nc.gpsimd.memset(shift_rows[:, 0, :], -BIG).then_inc(init_p, 1)
            nc.gpsimd.memset(shift_rows[:, 1, :], -1.0).then_inc(init_p, 1)
            nc.gpsimd.memset(maskop[:, :], 0.0).then_inc(init_p, 1)
            nc.gpsimd.memset(pick[:, :, :], 0.0).then_inc(init_p, 1)
            pool.wait_ge(init_p, 4)
            nc.gpsimd.affine_select(out=pick[:, :, :], in_=pick[:, :, :], compare_op=ALU.not_equal, fill=BIG,
                                    base=0, pattern=[[0, H], [-1, S]], channel_multiplier=1).then_inc(init_p, 1)
            nc.gpsimd.memset(ident[:, :], 0.0).then_inc(init_p, 1)
            nc.gpsimd.memset(ident16[:, :], 0.0).then_inc(init_p, 1)
            nc.gpsimd.memset(sel[:, :], 0.0).then_inc(init_p, 1)
            nc.gpsimd.memset(before_me[:, :, :], 1.0).then_inc(init_p, 1)
            nc.gpsimd.memset(mhalf[:, :], -0.5).then_inc(init_p, 1)
            nc.gpsimd.memset(keep[:, :], 1.0).then_inc(init_p, 1)
            pool.wait_ge(init_p, 11)
            for m in (ident, ident16):
                nc.gpsimd.affine_select(out=m[:, :], in_=m[:, :], compare_op=ALU.not_equal, fill=1.0,
                                        base=0, pattern=[[-1, 128]], channel_multiplier=1).then_inc(init_p, 1)
            nc.gpsimd.affine_select(out=sel[:, :].rearrange("p (g i) -> p g i", g=4),
                                    in_=sel[:, :].rearrange("p (g i) -> p g i", g=4),
                                    compare_op=ALU.not_equal, fill=1.0, base=-PR,
                                    pattern=[[-32, 4], [0, 32]], channel_multiplier=1).then_inc(init_p, 1)
            nc.gpsimd.affine_select(out=before_me[:, :, :], in_=before_me[:, :, :], compare_op=ALU.is_gt, fill=0.0,
                                    base=0, pattern=[[1, NE], [-1, NE]], channel_multiplier=0).then_inc(init_p, 1)
            linked = [0]

            def link(ins):
                linked[0] += 1
                ins.then_inc(pool_link, 1)

            def pool_links(s):
                return sum(2 * has_q(t) + has_a(t) for t in range(-1, s))

            def step(st):
                s = st.s
                if has_q(s) and s + 1 >= B:
                    pool.wait_ge(mask_in, st.at(lambda s: 16 * (mask_count(s) + 1)))
                    apart(pool)
                    for c in range(CH):
                        pool.wait_ge(kop_in[c], st.at(b_total))
                        apart(pool)
                    if s + 1 > B:
                        pool.wait_ge(masksum_done, st.at(mask_count))
                        apart(pool)
                    nc.gpsimd.tensor_scalar(maskop[:, :], maskin[:, :], 0, -BIG, ALU.is_equal, ALU.mult
                                            ).then_inc(mask_done, 1)
                if has_q(s):
                    pool.wait_ge(statq_done, st.at(lambda s: q_count(s) + 1))
                    apart(pool)
                    nc.gpsimd.tensor_scalar(veq[:, :], mvq[:, 1:2], EPS, None, ALU.add).then_inc(pool_link, 1)
                    pool.wait_ge(pool_link, st.at(lambda s: pool_links(s) + 1))
                    nc.gpsimd.tensor_tensor(rsq[:, :], veq[:, :], mhalf[:, :], ALU.pow).then_inc(pool_link, 1)
                    pool.wait_ge(pool_link, st.at(lambda s: pool_links(s) + 2))
                    if s + 1 >= B:
                        pool.wait_ge(keep_done, st.at(lambda s: mask_count(s) + 1))
                    nc.gpsimd.tensor_tensor(rkq[:, :], rsq[:, :], keep[:, :], ALU.mult).then_inc(rstdq_done, 1)
                if has_a(s):
                    n = 2 * has_q(s) + 1
                    pool.wait_ge(statf_done, st.at(lambda s: a_count(s) + 1))
                    apart(pool)
                    nc.gpsimd.tensor_scalar(vef[:, :], mvf[:, 1:2], EPS, None, ALU.add).then_inc(pool_link, 1)
                    pool.wait_ge(pool_link, st.at(lambda s: pool_links(s) + n))
                    nc.gpsimd.tensor_tensor(rsf[:, :], vef[:, :], mhalf[:, :], ALU.pow).then_inc(rstdf_done, 1)

            run_steps(pool, step)

        @block.scalar
        def _(act):
            act.wait_ge(w_in, 48)
            nc.scalar.activation(gains[:, :], bc[:, GX:GX + 4], ACT.Tanh).then_inc(init_a, 1)
            act.wait_ge(init_v, 7)

            def exps(st, kt):
                slot = kt % RING
                for h in range(2):
                    act.wait_ge(st_ready, st.at(lambda s: 2 * (KT * (s - 1) + kt) + h + 1))
                    if st.s > 1 or kt >= RING:
                        if h == 0:
                            act.wait_ge(av_done, st.at(lambda s: KT * (s - 1) + kt - RING + 1))
                    nc.scalar.activation(P[0:KP, slot, h * 4 * T:(h + 1) * 4 * T], pST[0:KP, h, 0:4 * T], ACT.Exp,
                                         scale=EXP_SCALE).then_inc(exp_done, 1)

            def step(st):
                s = st.s
                for kt in range(KT):
                    if has_e(s):
                        exps(st, kt)
                    for use in [u[1] for u in kv_uses(s) if u[0] == kt]:
                        c = int(use[1])
                        act.wait_ge(kv_ready, st.at(lambda s: upto(kv_uses, s, use)))
                        if use[0] == "k":
                            if s >= 0:
                                act.wait_ge(kop_in[c], st.at(lambda s: b_total(s)))
                            nc.scalar.activation(khi[:, c * CW:(c + 1) * CW], pKV[:, 0:CW], ACT.Identity,
                                                 bias=w(f"bk{layer_of(s + 1)}"), scale=1.0).then_inc(khi_done, 1)
                        else:
                            if s >= 2:
                                act.wait_ge(av_done, st.at(lambda s: KT * (s - 1)))
                            nc.scalar.activation(
                                V[0:KP, s % 2, 4 * c:4 * c + 4, :, 0:PR].rearrange("k t p i -> k (t p) i"),
                                pKV[0:KP, :].rearrange("k (m i) -> k m i", i=PR), ACT.Copy).then_inc(kv_free, 1)
                    if kt == 2 and has_q(s) and s + 1 >= B:
                        act.wait_ge(mask_done, st.at(lambda s: mask_count(s) + 1))
                        nc.scalar.activation(masksink[:, :], maskop[:, :], ACT.Copy, accum_out=masksum[:, :]
                                             ).then_inc(masksum_done, 1)
                    if kt == 6 and has_a(s):
                        act.wait_ge(logit_done, st.at(lambda s: a_count(s) + 1))
                        if layer_of(s - 2) == 0:
                            nc.scalar.activation(ge[:, :], lg[:, :], ACT.Exp, bias=lneg[:, :], scale=1.0,
                                                 accum_out=gse[:, :]).then_inc(gexp_done, 1)
                        else:
                            nc.scalar.activation(ge[:, :], lg[:, :], ACT.Exp, scale=-1.0).then_inc(gexp_done, 1)
                    if kt == 3 and has_f(s):
                        if layer_of(s - 3) == 0:
                            act.wait_ge(fh_free, st.at(lambda s: upto(fh_uses, s, "h7", True)))
                            nc.scalar.activation(HR[:, :, :], HR[:, :, :], ACT.Gelu).then_inc(gelu_done, 2)
                        else:
                            act.wait_ge(fh_free, st.at(lambda s: before(fh_uses, s, True)))
                            nc.scalar.activation(HR[:, 0:4, :], HR[:, 0:4, :], ACT.Gelu).then_inc(gelu_done, 1)
                            nc.scalar.activation(HR[0:F1, 4, :], HR[0:F1, 4, :], ACT.Gelu).then_inc(gelu_done, 1)

            run_steps(act, step)

        @block.vector
        def _(dve):
            nc.vector.memset(qmax[:, :, :, :, :].rearrange("p b r j q -> p (b r j q)"), 0.0).then_inc(init_v, 1)
            nc.vector.memset(ones[:, :], 1.0).then_inc(init_v, 1)
            dve.wait_ge(w_in, 48)
            nc.vector.tensor_scalar(bq_row[:, :], bq_row[:, :], QK_SCALE, None, ALU.mult).then_inc(init_v, 1)
            for l in range(LAYERS):
                a = COLS[f"wq{l}"][0]
                nc.vector.tensor_scalar(W[:, a:a + 2 * D], W[:, a:a + 2 * D], QK_SCALE, None, ALU.mult).then_inc(init_v, 1)
            a = COLS["bk0"][0]
            nc.vector.tensor_scalar(W[:, a:a + 2], W[:, a:a + 2], QK_SCALE, None, ALU.mult).then_inc(init_v, 1)
            Vf = V[:, :, :, :, :].rearrange("k b t p i -> k (b t p) i")
            nc.vector.memset(Vf[:, :, PR:PR + 1], 1.0).then_inc(init_v, 1)
            nc.vector.memset(Vf[:, :, PR + 1:32], 0.0).then_inc(init_v, 1)
            nc.vector.memset(woE[:, :, :, :], 0.0).then_inc(init_w, 1)
            nc.vector.memset(bvE[:, :, :], 0.0).then_inc(init_w, 1)
            nc.vector.memset(b2x[:, 0, :], 0.0).then_inc(init_w, 1)
            nc.vector.memset(gate[:, NE:NE + 1], 1.0).then_inc(init_v, 1)
            dve.wait_ge(init_p, 15)
            ig = ident[:, :].rearrange("p (g i) -> p g i", g=4)
            for k, (a, b) in enumerate(((0, HD), (HD, PR), (PR, PR + 1))):
                nc.vector.tensor_reduce(rowmask[:, k:k + 1], ig[:, :, a:b], AX.XY, ALU.add).then_inc(init_v, 1)
            dve.wait_ge(init_v, 12)
            dve.wait_ge(wo_in, 16 * 16)
            for j in range(2):
                for l in range(LAYERS):
                    for r in range(2):
                        nc.vector.tensor_scalar(bvm[:, l, r, j, :], ones[:, 0:S], rowmask[:, j:j + 1],
                                                bvE[:, l, r:r + 1], ALU.mult, ALU.mult).then_inc(init_v, 1)
                    if l == 0:
                        nc.vector.tensor_scalar(headmask[:, :, j, :], ones[:, :].rearrange("p (r q) -> p r q", r=2),
                                                rowmask[:, j:j + 1], rowmask[:, 2:3], ALU.mult, ALU.add).then_inc(init_v, 1)
            dve.wait_ge(init_a, 1)
            for l in range(LAYERS):
                nc.vector.tensor_scalar(tbo[:, l, :], bc[0:T, BO + l * D:BO + (l + 1) * D], gains[0:T, l:l + 1], None,
                                        ALU.mult).then_inc(init_v, 1)
            dve.wait_ge(init_v, 24)
            dve.wait_ge(x_in, 16)

            def links_before(s):
                return sum(links(t) for t in range(-1, s))

            def step(st):
                s = st.s
                linked = [0]

                def link(ins, alone=False):
                    linked[0] += 1
                    k = linked[0]
                    ins.then_inc(dve_link, 1)
                    dve.wait_ge(dve_link, st.at(lambda s: links_before(s) + k))
                    if alone:
                        apart(dve)

                def fy(name):
                    dve.wait_ge(fy_ready, st.at(lambda s: upto(fy_uses, s, name)))

                def fh(name):
                    dve.wait_ge(fh_ready, st.at(lambda s: upto(fh_uses, s, name)))

                def xg(f):
                    v = st.at(lambda s: D * (f(s) % G))
                    return X[:, bass.ds(v, D)] if st.turn is not None else X[:, v:v + D]

                for kt in range(KT):
                    if kt == 0 and has_tail(s):
                        dve.wait_ge(av_done, st.at(lambda s: KT * (s - 1)))
                        nc.vector.tensor_tensor(OM[:, s % 2, :], pO[:, 0:2 * T],
                                                headmask[:, :, :, :].rearrange("p r j q -> p (r j q)"),
                                                ALU.mult).then_inc(o_free, 1)
                    if has_m(s) and kt < NMAX // MAXES_PER_KT:
                        for m in range(MAXES_PER_KT * kt, MAXES_PER_KT * (kt + 1)):
                            dve.wait_ge(mx_ready, st.at(lambda s: NMAX * s + m + 1))
                            nc.vector.tensor_reduce(mx[:, s % 2, m // PAIRS, m % PAIRS:m % PAIRS + 1],
                                                    pMX[0:T, m % 2, 0:CW], AX.X, ALU.max).then_inc(max_done, 1)
                    for use in [u[1] for u in kv_uses(s) if u[0] == kt and u[1][0] == "k"]:
                        c = int(use[1])
                        dve.wait_ge(khi_done, st.at(lambda s: CH * (s + 1) + c + 1))
                        nc.vector.scalar_tensor_tensor(
                            out=klo[:, c * CW:(c + 1) * CW], in0=pKV[:, 0:CW], scalar=w(f"bk{layer_of(s + 1)}"),
                            in1=khi[:, c * CW:(c + 1) * CW], op0=ALU.add, op1=ALU.subtract).then_inc(kv_free, 1)

                    if has_q(s) and kt == 1:
                        if s + 1 >= B:
                            dve.wait_ge(x_done, st.at(lambda s: (s + 1 - B) // 2 + 1))
                        link(nc.vector.bn_stats(stq[:, :], xg(lambda s: (s + 1) // 2)), alone=True)
                        nc.vector.bn_aggr(mvq[:, :], stq[:, :]).then_inc(statq_done, 1)
                    if has_q(s) and s + 1 >= B and kt == 3:
                        dve.wait_ge(masksum_done, st.at(lambda s: mask_count(s) + 1))
                        nc.vector.tensor_scalar(keep[:, :], masksum[:, :], -BIG * (S2 - 0.5), None, ALU.is_gt
                                                ).then_inc(keep_done, 1)
                    if has_q(s) and kt == 4:
                        dve.wait_ge(rstdq_done, st.at(lambda s: q_count(s) + 1))
                        nc.vector.tensor_scalar(xnq[:, :], xg(lambda s: (s + 1) // 2), mvq[:, 0:1], rkq[:, :],
                                                ALU.subtract, ALU.mult).then_inc(xnq_done, 1)
                    if has_q(s) and kt == 5:
                        fh("qT")
                        nc.vector.tensor_copy(xnqT[:, :], pFH[:, 0:T]).then_inc(fh_free, 1)
                        nc.vector.tensor_copy(keepT[:, :], pFH[0:1, 128:128 + T]).then_inc(fh_free, 1)
                    if has_q(s) and kt == 6:
                        fh("q")
                        if s > 0:
                            dve.wait_ge(qmax_in, st.at(lambda s: 96 * (s + 1)))
                        link(nc.vector.tensor_copy(qhi[:, :], pFH[:, 0:T]))
                        nc.vector.tensor_tensor(qlo[:, :], pFH[:, 0:T], qhi[:, :], ALU.subtract).then_inc(fh_free, 1)

                    if has_a(s):
                        l = layer_of(s - 2)
                        grp = lambda s: (s - 3) // 2
                        if kt == 2:
                            fy("sum")
                            nc.vector.reciprocal(rden[:, :], pFY[:, 0:4 * T]).then_inc(fy_free, 1)
                            dve.wait_ge(fy_free, st.at(lambda s: upto(fy_uses, s, "sum", True)))
                            link(nc.vector.tensor_tensor(ON0[:, :], OM[:, :, :].rearrange("p b n -> p (b n)"), rden[:, :],
                                                         ALU.mult))
                            nc.vector.tensor_tensor(
                                ON[:, :, :, :, :].rearrange("p r j b q -> p b (r j) q"),
                                ON0[:, :].rearrange("p (b n q) -> p b n q", b=2, q=S),
                                bvm[:, l, :, :, :].rearrange("p r j q -> p (r j) q").unsqueeze(1).broadcast_to([128, 2, 4, S]),
                                ALU.add).then_inc(on_done, 1)
                        if kt == 3:
                            fy("y")
                            nc.vector.scalar_tensor_tensor(out=XF0[:, :], in0=pFY[0:T, 0:D], scalar=gains[0:T, l:l + 1],
                                                           in1=xg(grp), op0=ALU.mult, op1=ALU.add).then_inc(fy_free, 1)
                            dve.wait_ge(fy_free, st.at(lambda s: upto(fy_uses, s, "y", True)))
                            link(nc.vector.tensor_tensor(XF[:, :], XF0[:, :], tbo[:, l, :], ALU.add))
                            link(nc.vector.bn_stats(stf[:, :], XF[:, :]), alone=True)
                            nc.vector.bn_aggr(mvf[:, :], stf[:, :]).then_inc(statf_done, 1)
                        if kt == 4:
                            dve.wait_ge(rstdf_done, st.at(lambda s: a_count(s) + 1))
                            nc.vector.tensor_scalar(xnf[:, :], XF[:, :], mvf[:, 0:1], rsf[:, :],
                                                    ALU.subtract, ALU.mult).then_inc(xnf_done, 1)
                        if kt == 5:
                            fy("xT")
                            nc.vector.tensor_copy(xnfT[:, :], pFY[:, 0:T]).then_inc(fy_free, 1)

                        if kt == 6:
                            fy("lg")
                            ins = nc.vector.tensor_copy(lg[:, :], pFY[0:T, 0:NE]).then_inc(fy_free, 1)
                            dve.wait_ge(fy_free, st.at(lambda s: upto(fy_uses, s, "lg", True)))
                            if l == 0:
                                link(nc.vector.tensor_reduce(lmax[:, :], lg[:, :], AX.X, ALU.max))
                            nc.vector.tensor_scalar(lneg[:, :], lmax[:, :] if l == 0 else lg[:, 0:1], -1.0, None,
                                                    ALU.mult).then_inc(logit_done, 1)
                        if kt == 7:
                            dve.wait_ge(gexp_done, st.at(lambda s: a_count(s) + 1))
                            if l == 0:
                                link(nc.vector.reciprocal(g1[:, 0:1], gse[:, :]))
                                link(nc.vector.tensor_scalar(gp[:, :], ge[:, :], g1[:, 0:1], None, ALU.mult))
                            else:
                                link(nc.vector.tensor_scalar(g1[:, :], ge[:, :], 1.0, None, ALU.add))
                                link(nc.vector.reciprocal(g2[:, :], g1[:, :]))
                                link(nc.vector.tensor_scalar(gp[:, :], g2[:, :], bc[0:T, RS:RS + 1], None, ALU.mult))
                            pj = gp[:, :].unsqueeze(1).broadcast_to([T, NE, NE])
                            pe_ = gp[:, :].unsqueeze(2).broadcast_to([T, NE, NE])
                            nc.vector.tensor_tensor(ggt[:, :, :], pj, pe_, ALU.is_gt)
                            link(nc.vector.tensor_tensor(geq[:, :, :], pj, pe_, ALU.is_equal))
                            link(nc.vector.tensor_tensor(gel[:, :, :], geq[:, :, :], before_me[:, :, :], ALU.mult))
                            link(nc.vector.tensor_tensor(grk[:, :, :], gel[:, :, :], ggt[:, :, :], ALU.add))
                            link(nc.vector.tensor_reduce(rank[:, :], grk[:, :, :], AX.X, ALU.add))
                            link(nc.vector.scalar_tensor_tensor(out=gsp[:, :], in0=rank[:, :], scalar=1.5, in1=gp[:, :],
                                                                op0=ALU.is_lt, op1=ALU.mult))
                            link(nc.vector.tensor_reduce(gden[:, :], gsp[:, :], AX.X, ALU.add))
                            link(nc.vector.reciprocal(grd[:, :], gden[:, :]))
                            nc.vector.tensor_scalar(gate[:, 0:NE], gsp[:, :], grd[:, :], None, ALU.mult).then_inc(gate_done, 1)
                        if kt == 10:
                            fy("gT")
                            nc.vector.tensor_copy(gateT[:, :], pFY[0:NE + 1, 0:T]).then_inc(fy_free, 1)
                    if has_a(s) or has_f(s):
                        l = layer_of(s - 2 if has_a(s) else s - 3)
                        for use in [u[1] for u in fh_uses(s) if u[0] == kt and u[1][0] == "h"]:
                            e = int(use[1:])
                            fh(use)
                            if l == 0:
                                nc.vector.tensor_tensor(
                                    HR[:, F0C * e:F0C * (e + 1), :], pFH[:, 0:F0C * T].rearrange("p (c t) -> p c t", c=F0C),
                                    w("b1_0")[:, F0C * e:F0C * (e + 1)].unsqueeze(2).broadcast_to([128, F0C, T]),
                                    ALU.add).then_inc(fh_free, 1)
                            elif e == 0:
                                nc.vector.tensor_tensor(
                                    HR[:, 0:4, :], pFH[:, 0:4 * T].rearrange("p (c t) -> p c t", c=4),
                                    w("b1_1").unsqueeze(2).broadcast_to([128, 4, T]), ALU.add).then_inc(fh_free, 1)
                            else:
                                nc.vector.tensor_scalar(HR[0:F1, 4, :], pFH[0:F1, 0:T], bs1b[:, 0:1], None, ALU.add
                                                        ).then_inc(fh_free, 1)
                    if has_f(s) and 4 <= kt <= 7:
                        i = kt - 4
                        fy(f"y{i}")
                        for j, e in enumerate(experts_of(i)):
                            y = pFY[0:T, j * D:(j + 1) * D]
                            if e == 0:
                                ins = nc.vector.tensor_scalar(acc[:, 0, :], y, gate[:, 0:1], None, ALU.mult)
                            else:
                                ins = nc.vector.scalar_tensor_tensor(out=acc[:, j, :], in0=y, scalar=gate[:, e:e + 1],
                                                                     in1=acc[:, 1 - j, :], op0=ALU.mult, op1=ALU.add)
                            if j:
                                ins.then_inc(fy_free, 1)
                                dve.wait_ge(fy_free, st.at(lambda s: upto(fy_uses, s, f"y{i}", True)))
                            else:
                                link(ins)
                    if has_f(s) and kt == 8:
                        l = layer_of(s - 3)
                        fy("yb")
                        nc.vector.tensor_tensor(acc[:, 0, :], pFY[0:T, 0:D], acc[:, 1, :], ALU.add).then_inc(fy_free, 1)
                        dve.wait_ge(fy_free, st.at(lambda s: upto(fy_uses, s, "yb", True)))
                        nc.vector.scalar_tensor_tensor(out=xg(lambda s: (s - 4) // 2), in0=acc[:, 0, :],
                                                       scalar=gains[0:T, 2 + l:3 + l], in1=XF[:, :],
                                                       op0=ALU.mult, op1=ALU.add).then_inc(x_done, 1)

                    if has_m(s) and kt == 8:
                        dve.wait_ge(max_done, st.at(lambda s: NMAX * (s + 1)))
                        link(nc.vector.tensor_reduce(m8[:, :], mx[:, s % 2, :, :].rearrange("t c p -> t p c"), AX.X, ALU.max))
                        if s > 0:
                            dve.wait_ge(fy_ready, st.at(lambda s: upto(fy_uses, s - 1, "ct")))
                        link(nc.vector.tensor_scalar(cc[:, 0, :], m8[:, :], 1.0 / BIG, None, ALU.mult))
                        nc.vector.scalar_tensor_tensor(out=cc[:, 1, :], in0=cc[:, 0, :], scalar=-BIG, in1=m8[:, :],
                                                       op0=ALU.mult, op1=ALU.add).then_inc(cc_ready, 1)
                    if has_m(s) and kt == 9:
                        fy("ct")
                        if s > 0:
                            dve.wait_ge(shift_in, st.at(lambda s: 16 * s))
                        nc.vector.tensor_copy(ct[:, :], pFY[0:2 * PAIRS, 0:T // 2].bitcast(F16)).then_inc(fy_free, 1)
                assert linked[0] == links(s), (s, linked[0], links(s))

            run_steps(dve, step)

        @block.tensor
        def _(pe):
            pe.wait_ge(init_v, 24)
            pe.wait_ge(init_p, 15)
            pe.wait_ge(init_dma, 128)
            pe.wait_ge(f_in, 16 * 8)

            def score_tile(st, kt):
                b = (st.s - 1) % 2
                if kt == 0:
                    pe.wait_ge(qexp_in[b], st.at(lambda s: 16 * ((s - 1) // 2 + 1)))
                    pe.wait_ge(shift_in, st.at(lambda s: 16 * s))
                for h in range(2):
                    if st.s > 1 or kt > 0:
                        pe.wait_ge(exp_done, st.at(lambda s: 2 * (KT * (s - 1) + kt) + h - 1))
                    for i in range(4):
                        p = 4 * h + i
                        mm = nc.tensor.matmul(pST[0:KP, h, i * T:(i + 1) * T],
                                              kop[0:ROWS, b, p, kt * KP:(kt + 1) * KP],
                                              qexp[0:ROWS, b, p, :, :].rearrange("r j q -> r (j q)"),
                                              start=True, stop=True)
                    mm.then_inc(st_ready, 1)

            def weigh(st, lag, kt):
                b = (st.s - lag) % 2
                if kt == 0:
                    pe.wait_ge(kv_free, st.at(lambda s: upto(kv_uses, s - 1, "v2", True)))
                    if st.s > 1:
                        pe.wait_ge(o_free, st.at(lambda s: s - 1))
                for r in range(2):
                    pe.wait_ge(exp_done, st.at(lambda s: 2 * (KT * (s - lag) + kt) + r + 1))
                    for g in range(4):
                        p = 4 * r + g
                        mm = nc.tensor.matmul(pO[32 * g:32 * (g + 1), r * T:(r + 1) * T],
                                              V[0:KP, b, kt, p, :], P[0:KP, kt % RING, p * T:(p + 1) * T],
                                              start=(kt == 0 and r == 0), stop=(kt == KT - 1), skip_group_check=True)
                mm.then_inc(av_done, 1)

            def max_scores(st, m):
                c, p = divmod(m, PAIRS)
                if m == 0:
                    pe.wait_ge(qmax_in, st.at(lambda s: 96 * (s + 1)))
                if p == 0:
                    pe.wait_ge(kop_in[c], st.at(b_total))
                if st.s > 0 or m > 1:
                    pe.wait_ge(max_done, st.at(lambda s: NMAX * s + m - 1))
                nc.tensor.matmul(pMX[0:T, m % 2, 0:CW],
                                 qmax[0:SHIFT0, st.s % 2, p, :, :].rearrange("r j q -> r (j q)"),
                                 kop[0:SHIFT0, st.s % 2, p, c * CW:(c + 1) * CW], start=True, stop=True
                                 ).then_inc(mx_ready, 1)

            def step(st):
                s = st.s

                def free(sem_, uses, name):
                    first = before(uses, s) == 0 and uses(s)[0][1] == name
                    if not first:
                        def n(s):
                            u = [x for x in uses(s) if x[1] == name][0]
                            return upto(uses, s, name, True) - u[2]
                        pe.wait_ge(sem_, st.at(n))

                for kt in range(KT):
                    if has_e(s):
                        score_tile(st, kt)
                    if has_tail(s) and kt == 0:
                        weigh(st, 2, KT - 2)
                        weigh(st, 2, KT - 1)
                    if has_e(s) and kt >= 2:
                        weigh(st, 1, kt - 2)
                    if has_m(s) and kt < NMAX // MAXES_PER_KT:
                        for m in range(MAXES_PER_KT * kt, MAXES_PER_KT * (kt + 1)):
                            max_scores(st, m)

                    for use in [u[1] for u in kv_uses(s) if u[0] == kt]:
                        c = int(use[1])
                        free(kv_free, kv_uses, use)
                        if use[0] == "k":
                            if c == 0:
                                pe.wait_ge(c_in[(s + 1) % 2], st.at(lambda s: 16 * ((s + 1) // 2 + 1)))
                            nc.tensor.matmul(pKV[:, 0:CW], w(f"wk{layer_of(s + 1)}"),
                                             C[:, (s + 1) % 2, c * CW:(c + 1) * CW], start=True, stop=True
                                             ).then_inc(kv_ready, 1)
                        else:
                            for i in range(4):
                                t = 4 * c + i
                                mm = nc.tensor.matmul(pKV[0:KP, i * D:(i + 1) * D], C[:, s % 2, t * KP:(t + 1) * KP],
                                                      w(f"wv{layer_of(s)}"), start=True, stop=True)
                            mm.then_inc(kv_ready, 1)

                    for use in [u[1] for u in fh_uses(s) if u[0] == kt]:
                        free(fh_free, fh_uses, use)
                        if use == "qT":
                            pe.wait_ge(xnq_done, st.at(lambda s: q_count(s) + 1))
                            nc.tensor.transpose(pFH[:, 0:T], xnq[:, :], ident[0:T, 0:T])
                            nc.tensor.transpose(pFH[0:1, 128:128 + T], keep[:, :], ident[0:T, 0:T]).then_inc(fh_ready, 1)
                        elif use == "q":
                            l = layer_of(s + 1)
                            nc.tensor.matmul(pFH[:, 0:T], w(f"wq{l}"), xnqT[:, :], start=True, stop=False)
                            nc.tensor.matmul(pFH[:, 0:T], bq_row[:, l * D:(l + 1) * D], keepT[:, :],
                                             start=False, stop=True).then_inc(fh_ready, 1)
                        else:
                            e = int(use[1:])
                            l = layer_of(s - 2 if s % 2 else s - 3)
                            if l == 0:
                                for c in range(F0C):
                                    mm = nc.tensor.matmul(pFH[:, c * T:(c + 1) * T], w1a[:, e, c * 128:(c + 1) * 128],
                                                          xnfT[:, :], start=True, stop=True)
                            elif e == 0:
                                for c in range(4):
                                    mm = nc.tensor.matmul(
                                        pFH[:, c * T:(c + 1) * T],
                                        w1b[:, 2 * c:2 * c + 2, :].rearrange("d e f -> d (e f)"),
                                        xnfT[:, :], start=True, stop=True)
                            else:
                                mm = nc.tensor.matmul(pFH[0:F1, 0:T], w("ws1"), xnfT[:, :], start=True, stop=True)
                            mm.then_inc(fh_ready, 1)

                    for use in [u[1] for u in fy_uses(s) if u[0] == kt]:
                        free(fy_free, fy_uses, use)
                        if use == "sum":
                            pe.wait_ge(o_free, st.at(lambda s: s - 1))
                            mm = nc.tensor.matmul(pFY[:, 0:4 * T], sel[:, :], OM[:, :, :].rearrange("p b n -> p (b n)"),
                                                  start=True, stop=True)
                        elif use == "y":
                            pe.wait_ge(on_done, st.at(lambda s: a_count(s) + 1))
                            l = layer_of(s - 2)
                            for r in range(2):
                                for j in range(2):
                                    mm = nc.tensor.matmul(pFY[0:T, 0:D], ON[:, r, j, :, :].rearrange("p b q -> p (b q)"), woE[:, l, r, :],
                                                          start=(r == 0 and j == 0), stop=(r == 1 and j == 1))
                        elif use == "xT":
                            pe.wait_ge(xnf_done, st.at(lambda s: a_count(s) + 1))
                            mm = nc.tensor.transpose(pFY[:, 0:T], xnf[:, :], ident[0:T, 0:T])
                        elif use == "lg":
                            mm = nc.tensor.matmul(pFY[0:T, 0:NE], xnfT[:, :], w(f"gate{layer_of(s - 2)}"),
                                                  start=True, stop=True)
                        elif use == "gT":
                            pe.wait_ge(gate_done, st.at(lambda s: a_count(s) + 1))
                            mm = nc.tensor.transpose(pFY[0:NE + 1, 0:T], gate[:, :], ident[0:T, 0:T])
                        elif use == "ct":
                            pe.wait_ge(cc_ready, st.at(lambda s: s + 1))
                            mm = nc.tensor.transpose(pFY[0:2 * PAIRS, 0:T // 2].bitcast(F16),
                                                     cc[:, :, :].rearrange("t i p -> t (i p)"), ident16[0:T, 0:T])
                        elif use == "yb":
                            l = layer_of(s - 3)
                            if l == 1:
                                nc.tensor.matmul(pFY[0:T, 0:D], HR[0:F1, 4, :], ws2b[:, :], start=True, stop=False)
                            mm = nc.tensor.matmul(pFY[0:T, 0:D], gateT[:, :], b2x[:, l, :], start=(l == 0), stop=True)
                        else:
                            if use == "y0":
                                pe.wait_ge(gelu_done, st.at(lambda s: 2 * (f_count(s) + 1)))
                            l = layer_of(s - 3)
                            i = int(use[1])
                            for j, e in enumerate(experts_of(i)):
                                o = pFY[0:T, j * D:(j + 1) * D]
                                if l == 0:
                                    for c in range(F0C):
                                        mm = nc.tensor.matmul(o, HR[:, F0C * e + c, :], w2a[:, e, c, :],
                                                              start=(c == 0), stop=(c == F0C - 1))
                                else:
                                    half = slice(F1 * (e % 2), F1 * (e % 2 + 1))
                                    mm = nc.tensor.matmul(o, HR[half, e // 2, :], w2b[half, e // 2, :],
                                                          start=True, stop=True)
                        mm.then_inc(fy_ready, 1)

            run_steps(pe, step)


def kernel(**inputs):
    import numpy as np
    import concourse.bacc as bacc
    from concourse.bass_utils import run_bass_kernel_spmd

    def arr(name):
        return np.asarray(inputs[name])

    def pairs_last(a):
        return a.reshape(a.shape[:-1] + (PAIRS, PR)).swapaxes(-1, -2).reshape(a.shape)

    x0 = arr("x")
    wq = [arr("L0_xattn_Wq").T, arr("L1_xattn_wq_kernel")]
    wk = [arr("L0_xattn_Wk").T, arr("L1_xattn_wk_kernel")]
    wv = [arr("L0_xattn_Wv").T, arr("L1_xattn_wv_kernel")]
    parts = {"bk0": pairs_last(arr("L0_xattn_bk"))[:, None], "bk1": pairs_last(arr("L1_xattn_wk_bias"))[:, None],
             "gate0": arr("L0_ffn_gate_w"), "gate1": arr("L1_ffn_gate_W"),
             "b1_0": arr("L0_ffn_b1").reshape(E0 * F0C, 128).T, "b1_1": arr("L1_ffn_b1").reshape(-1, 128).T,
             "ws1": arr("L1_ffn_Ws1")}
    for l in range(LAYERS):
        parts[f"wq{l}"], parts[f"wk{l}"], parts[f"wv{l}"] = pairs_last(wq[l]), pairs_last(wk[l]), wv[l]
    arrays = {
        "x": x0.reshape(B * S, D),
        "ctxT": arr("ctx_1024").transpose(0, 2, 1),
        "mask": arr("mask_BxSxS2_ik1").reshape(G, T, S2),
        "wpack": np.concatenate([parts[n] for n in COLS], axis=1),
        "bqrow": np.concatenate([pairs_last(arr("L0_xattn_bq")), pairs_last(arr("L1_xattn_wq_bias"))])[None],
        "bcast": np.concatenate([arr("L0_xattn_bo"), arr("L1_xattn_wo_bias"), arr("g_xattn"), arr("g_ffn"),
                                 arr("L1_ffn_route_scale").reshape(1)]),
        "wo": np.stack([arr("L0_xattn_Wo").T, arr("L1_xattn_wo_kernel")]),
        "bvc": np.stack([arr("L0_xattn_bv"), arr("L1_xattn_wv_bias")]).reshape(LAYERS, 2, 4, PR).transpose(0, 2, 3, 1),
        "w1_0": arr("L0_ffn_w1"), "w2_0": arr("L0_ffn_w2"), "b2_0": arr("L0_ffn_b2"),
        "w1_1": arr("L1_ffn_W1"), "w2_1": arr("L1_ffn_W2"),
        "b2_1": np.concatenate([arr("L1_ffn_b2"), arr("L1_ffn_bs2")[None]]),
        "ws2": arr("L1_ffn_Ws2"), "bs1": arr("L1_ffn_bs1")[:, None],
    }
    nc = bacc.Bacc("TRN2", target_bir_lowering=False, num_devices=1)
    given, args = {}, []
    for name, a in arrays.items():
        a = np.ascontiguousarray(a)
        given[f"in_{name}"] = a
        args.append(nc.dram_tensor(f"in_{name}", a.shape, mybir.dt.from_np(a.dtype), kind="ExternalInput").ap())
    args.append(nc.dram_tensor("out_0", (B * S, D), F32, kind="ExternalOutput").ap())
    build(nc, *args)
    r = run_bass_kernel_spmd(nc, [given], core_ids=[0])
    return r.results[0]["out_0"].reshape(B, S, D)
```

```python
from contextlib import ExitStack

import concourse.bass as bass
from concourse import mybir

ALU = mybir.AluOpType
ACT = mybir.ActivationFunctionType
AX = mybir.AxisListType
F32 = mybir.dt.float32
F16 = mybir.dt.float16
I32 = mybir.dt.int32

LAYERS = 2
B, S, D, S2 = 16, 56, 128, 1500
H = 16
HD = D // H
PAIRS = H // 2
PR = 2 * HD
G = B // 2
T = 2 * S
NB = LAYERS * B
KT, KP = 12, 125
CH, CW = 3, 500
KPC = CW // KP
MASK0 = 3 * PR
SHIFT0 = MASK0 + S
ROWS = SHIFT0 + 2
RING = 4
NMAX = CH * PAIRS
MAXES_PER_KT = NMAX // KT
E_LAG = 3
AV_LAG = E_LAG + 2
QK_SCALE = 4.0
EXP_SCALE = 1.0 / (QK_SCALE * QK_SCALE * float(HD) ** 0.5)
BIG = 32768.0
EPS = 1e-5
E0, F0C = 8, 4
E1, F1 = 8, 64
NE = 8

COLS = {}
_at = 0
for _name, _n in (("wq0", D), ("wk0", D), ("wv0", D), ("wq1", D), ("wk1", D), ("wv1", D),
                  ("bk0", 1), ("bk1", 1), ("gate0", NE), ("gate1", NE), ("b1_0", E0 * F0C),
                  ("b1_1", E1 * F1 // 128), ("ws1", F1)):
    COLS[_name] = (_at, _at + _n)
    _at += _n
NCOLS = _at
BO, GX, GF, RS, NBC = 0, 2 * D, 2 * D + 2, 2 * D + 4, 2 * D + 5


def has_k(s):
    return -1 <= s <= NB - 2


def has_v(s):
    return 0 <= s <= NB - 1


def has_m(s):
    return 0 <= s <= NB - 1


def has_q(s):
    return s % 2 == 1 and -1 <= s <= NB - 3


def has_a(s):
    return s % 2 == 1 and 3 <= s <= NB + 1


def has_f(s):
    return s % 2 == 0 and 4 <= s <= NB + 2


def has_end(s):
    return s % 2 == 1 and 5 <= s <= NB + 3


def has_mask(s):
    return s == 4 or s % 2 == 0 and B <= s <= NB - 4


def is_batch(n):
    return 0 <= n < NB


def layer_of(n):
    return n // B


def tile_at(kt, lag):
    return (1, kt - lag) if kt >= lag else (2, kt - lag + KT)


def kv_uses(s):
    uses = []
    if has_k(s):
        uses += [(2, "k0", 1), (4, "k1", 1), (6, "k2", 1)]
    if has_v(s):
        uses += [(8, "v0", 1), (9, "v1", 1), (10, "v2", 1)]
    return uses


def fh_uses(s):
    uses = []
    if has_q(s):
        uses += [(4, "qT", 2), (6, "q", 1)]
    if has_a(s):
        uses += [(10, "h0", 1), (11, "h1", 1)]
    if has_f(s) and layer_of(s - 3) == 0:
        uses += [(e - 2, f"h{e}", 1) for e in range(2, 8)]
    return uses


def fy_uses(s):
    uses = []
    if has_m(s - 1):
        uses.append((0, "ct", 1))
    if has_end(s):
        uses += [(1, "y3", 1), (3, "yb", 1)]
    if is_batch(s - 2):
        uses.append((5, "sum", 1))
    if has_a(s):
        uses += [(7, "y", 1), (9, "xT", 1), (10, "lg", 1)]
    if has_f(s):
        uses += [(7, "gT", 1)] + [(9 + i, f"y{i}", 1) for i in range(3)]
    return sorted(uses, key=lambda u: u[0])


def issued_before(uses, s, kt):
    if kt > 0:
        return [(0, u[1]) for u in uses(s) if u[0] == kt - 1]
    return [(1, u[1]) for u in uses(s - 1) if u[0] == KT - 1]


def experts_of(i):
    e = 4 * (i // 2) + i % 2
    return e, e + 2


def before(uses, s, freed=False):
    return sum(u[2] if freed else 1 for t in range(-1, s) for u in uses(t))


def upto(uses, s, name, freed=False):
    n = before(uses, s, freed)
    for u in uses(s):
        n += u[2] if freed else 1
        if u[1] == name:
            return n
    raise KeyError((s, name))


def links(s):
    n = 0
    if has_m(s - 1):
        n += 2
    if has_q(s):
        n += 2
    if has_a(s):
        n += 2 + (layer_of(s - 2) == 0)
    if has_f(s):
        n += 9 + (layer_of(s - 3) == 1) + 2
    if has_end(s):
        n += 2
    return n


def b_total(n):
    return 48 * min(n + 1, B) + 64 * max(0, n + 1 - B)


class Step:

    def __init__(self, s0, turn=None, turns=1):
        self.s, self.turn, self.turns = s0, turn, turns

    def at(self, f):
        v = f(self.s)
        if self.turn is None:
            return v
        d = f(self.s + 2) - v
        assert all(f(self.s + 2 * i) == v + i * d for i in range(self.turns))
        return v + self.turn * d if d else v


PEELED_AND_LOOPS = [-1, 0, 1, 2, 3, 4, (5, 5), 15, 16, 17, 18, 19, 20, (21, 4), 29, 30, 31, 32, 33, 34, 35]


def run_steps(eng, step):
    for item in PEELED_AND_LOOPS:
        if isinstance(item, tuple):
            s0, turns = item
            with eng.Fori(0, turns) as turn:
                step(Step(s0, turn, turns))
                step(Step(s0 + 1, turn, turns))
        else:
            step(Step(item))


def build(nc, x, ctxT, mask, wpack, bqrow, bcast, wo, bvc, w1_0, w2_0, b2_0, w1_1, w2_1, b2_1, ws2, bs1, out):
    with ExitStack() as ctx:
        def sb(name, shape, dt=F32):
            return ctx.enter_context(nc.sbuf_tensor(name, shape, dt))

        def ps(name, shape):
            return ctx.enter_context(nc.psum_tensor(name, shape, F32))

        def sem(name):
            return ctx.enter_context(nc.semaphore(name))

        W = sb("W", [128, NCOLS])

        def w(name):
            a, b = COLS[name]
            return W[:, a:b]

        bq_row = sb("bq_row", [1, LAYERS * D])
        bc = sb("bc", [128, NBC])
        gains = sb("gains", [128, 4])
        tbo = sb("tbo", [T, LAYERS, D])
        woE = sb("woE", [128, LAYERS, 2, D])
        bvE = sb("bvE", [128, LAYERS, 2])
        w1a = sb("w1a", [128, E0, F0C * 128])
        w2a = sb("w2a", [128, E0, F0C, D])
        w1b = sb("w1b", [128, E1, F1])
        w2b = sb("w2b", [128, E1 // 2, D])
        ws2b = sb("ws2b", [F1, D])
        bs1b = sb("bs1b", [F1, 1])
        b2x = sb("b2x", [NE + 1, LAYERS, D])
        ident = sb("ident", [128, 128])
        ident16 = sb("ident16", [128, 128], F16)
        sel = sb("sel", [128, 128])
        rowmask = sb("rowmask", [128, 4])
        headmask = sb("headmask", [128, 2, 2, S])
        bvm = sb("bvm", [128, LAYERS, 2, 2, S])
        ones = sb("ones", [128, T])
        before_me = sb("before_me", [T, NE, NE])
        mhalf = sb("mhalf", [T, 1])
        pick = sb("pick", [S, H, S], F16)

        X = sb("X", [T, G * D])
        C = sb("C", [128, 2, S2])
        khi = sb("khi", [128, S2], F16)
        klo = sb("klo", [128, S2], F16)
        kop = sb("kop", [128, 2, PAIRS, S2], F16)
        qmax = sb("qmax", [128, 2, PAIRS, 2, S], F16)
        qexp = sb("qexp", [128, 2, PAIRS, 2, S], F16)
        V = sb("V", [128, 2, KT, PAIRS, 32])
        P = sb("P", [128, RING, PAIRS * T])
        maskin = sb("maskin", [T, S2], I32)
        maskop = sb("maskop", [T, S2], F16)
        shift_rows = maskin[0:1, :].bitcast(F16).rearrange("a (i n) -> a i n", i=2)
        maskraw = sb("maskraw", [T, S2], F16)
        masksink = sb("masksink", [T, S2], F16)
        masksum = sb("masksum", [T, 1])
        keep = sb("keep", [T, 1])
        stq, mvq = sb("stq", [T, 6]), sb("mvq", [T, 2])
        stf, mvf = sb("stf", [T, 6]), sb("mvf", [T, 2])
        veq, rsq, rkq = sb("veq", [T, 1]), sb("rsq", [T, 1]), sb("rkq", [T, 1])
        vef, rsf = sb("vef", [T, 1]), sb("rsf", [T, 1])
        xnq = sb("xnq", [T, D])
        xnqT = sb("xnqT", [128, T])
        keepT = sb("keepT", [1, T])
        qhi = sb("qhi", [128, T], F16)
        qlo = sb("qlo", [128, T], F16)
        mx = sb("mx", [T, 2, CH, PAIRS])
        m8 = sb("m8", [T, PAIRS])
        cc = sb("cc", [T, 2, PAIRS], F16)
        ct = sb("ct", [2 * PAIRS, T], F16)
        OM = sb("OM", [128, 2, 2 * T])
        rden = sb("rden", [128, 2 * T])
        ON0 = sb("ON0", [128, 2 * T])
        ON = sb("ON", [128, 2, 2, 2, S])
        XF0, XF = sb("XF0", [T, D]), sb("XF", [T, D])
        xnf = sb("xnf", [T, D])
        xnfT = sb("xnfT", [128, T])
        lg = sb("lg", [T, NE])
        lmax, lneg = sb("lmax", [T, 1]), sb("lneg", [T, 1])
        ge, gse = sb("ge", [T, NE]), sb("gse", [T, 1])
        g1, g2 = sb("g1", [T, NE]), sb("g2", [T, NE])
        gp = sb("gp", [T, NE])
        ggt, geq, gel, grk = (sb(n, [T, NE, NE]) for n in ("ggt", "geq", "gel", "grk"))
        rank, gsp = sb("rank", [T, NE]), sb("gsp", [T, NE])
        gden, grd = sb("gden", [T, 1]), sb("grd", [T, 1])
        gate = sb("gate", [T, NE + 1])
        gateT = sb("gateT", [NE + 1, T])
        HR = sb("HR", [128, E0 * F0C, T])
        acc = sb("acc", [T, 2, D])

        pMX = ps("pMX", [128, 2, 512])
        pST = ps("pST", [128, 2, 512])
        pO = ps("pO", [128, 512])
        pKV = ps("pKV", [128, 512])
        pFH = ps("pFH", [128, 512])
        pFY = ps("pFY", [128, 512])

        w_in, x_in, f_in, wo_in = sem("w_in"), sem("x_in"), sem("f_in"), sem("wo_in")
        c_in = [sem("c_in0"), sem("c_in1")]
        mask_in = sem("mask_in")
        init_p = sem("init_p")
        init_v = sem("init_v")
        init_l = sem("init_l")
        init_w = sem("init_w")
        init_a = sem("init_a")
        init_dma = sem("init_dma")
        kop_in = [sem(f"kop_in{c}") for c in range(CH)]
        qmax_in = sem("qmax_in")
        qexp_in = [sem("qexp_in0"), sem("qexp_in1")]
        shift_in = sem("shift_in")
        mask_done, masksum_done, keep_done = sem("mask_done"), sem("masksum_done"), sem("keep_done")
        maskop_done = sem("maskop_done")
        khi_done = sem("khi_done")
        kv_ready, kv_free = sem("kv_ready"), sem("kv_free")
        mx_ready, max_done = sem("mx_ready"), sem("max_done")
        cc_ready = sem("cc_ready")
        st_ready, exp_done = sem("st_ready"), sem("exp_done")
        av_done, o_free = sem("av_done"), sem("o_free")
        fh_ready, fh_free = sem("fh_ready"), sem("fh_free")
        fy_ready, fy_free = sem("fy_ready"), sem("fy_free")
        statq_done, rstdq_done, xnq_done = sem("statq_done"), sem("rstdq_done"), sem("xnq_done")
        statf_done, rstdf_done, xnf_done = sem("statf_done"), sem("rstdf_done"), sem("xnf_done")
        on_done = sem("on_done")
        logit_done, gexp_done, gate_done = sem("logit_done"), sem("gexp_done"), sem("gate_done")
        gelu_done = sem("gelu_done")
        x_done = sem("x_done")
        dve_link, pool_link = sem("dve_link"), sem("pool_link")
        stored = sem("stored")
        passed = sem("passed")

        block = ctx.enter_context(nc.Block())

        def apart(eng):
            eng.sem_inc(passed, 1)

        def groups(f):
            return lambda s: sum(f(t) for t in range(-1, s))

        q_count, a_count, f_count = groups(has_q), groups(has_a), groups(has_f)

        mask_count = groups(lambda t: has_q(t) and t + 1 >= B)
        maskraw_count = groups(has_mask)

        @block.sync
        def _(sp):
            sp.dma_start(W[:, :], wpack).then_inc(w_in, 16)
            sp.dma_start(C[:, 0, :], ctxT[0]).then_inc(c_in[0], 16)
            sp.dma_start(X[:, :].rearrange("t (g d) -> t g d", g=G),
                         x.rearrange("(g t) d -> t g d", g=G)).then_inc(x_in, 16)
            sp.dma_start(bq_row[:, :], bqrow).then_inc(w_in, 16)
            sp.dma_start(bc[:, :], bcast.partition_broadcast(128)).then_inc(w_in, 16)
            sp.wait_ge(init_v, 1)
            sp.wait_ge(init_p, 5)
            for b in range(2):
                sp.dma_start(kop[MASK0:SHIFT0, b, :, :],
                             maskop[0:S, :].unsqueeze(1).broadcast_to([S, PAIRS, S2])).then_inc(init_dma, 16)
                for i in range(2):
                    sp.dma_start(kop[SHIFT0 + i:SHIFT0 + i + 1, b, :, :],
                                 shift_rows[:, i:i + 1, :].broadcast_to([1, PAIRS, S2])).then_inc(init_dma, 16)
                sp.dma_start(qmax[MASK0:SHIFT0, b, :, :, :],
                             pick[:, :, :].rearrange("s (p j) q -> s p j q", j=2)).then_inc(init_dma, 16)

            def late_loads():
                sp.dma_start(C[:, 1, :], ctxT[1]).then_inc(c_in[1], 16)
                sp.wait_ge(init_w, 3)
                for l in range(LAYERS):
                    for g in range(4):
                        sp.dma_start(woE[32 * g:32 * g + PR, l, :, :],
                                     wo[l].rearrange("(r g i) n -> g i r n", r=2, g=4)[g]).then_inc(wo_in, 16)
                        sp.dma_start(bvE[32 * g:32 * g + PR, l, :], bvc[l, g]).then_inc(wo_in, 16)
                sp.dma_start(w1a[:, :, :], w1_0.rearrange("e d f -> d e f")).then_inc(f_in, 16)
                sp.dma_start(w2a[:, :, :, :], w2_0.rearrange("e (c f) d -> f e c d", c=F0C)).then_inc(f_in, 16)
                sp.dma_start(w1b[:, :, :], w1_1.rearrange("e d f -> d e f")).then_inc(f_in, 16)
                sp.dma_start(w2b[:, :, :], w2_1.rearrange("(c e) f d -> (e f) c d", e=2)).then_inc(f_in, 16)
                sp.dma_start(b2x[0:NE, 0, :], b2_0).then_inc(f_in, 16)
                sp.dma_start(b2x[:, 1, :], b2_1).then_inc(f_in, 16)
                sp.dma_start(ws2b[:, :], ws2).then_inc(f_in, 16)
                sp.dma_start(bs1b[:, :], bs1).then_inc(f_in, 16)
                sp.wait_ge(init_dma, 128)
                sp.dma_start(maskin[:, :], mask[0]).then_inc(mask_in, 16)

            def key_chunk(st, ahead, c):
                n, cols = st.s + ahead, slice(c * CW, (c + 1) * CW)
                dst = n % 2
                sp.wait_ge(kv_free, st.at(lambda s: upto(kv_uses, s + ahead - 1, f"k{c}", True)))
                apart(sp)
                if n >= 2:
                    sp.wait_ge(st_ready, st.at(lambda s: 2 * (KT * (s + ahead - 2) + KPC * (c + 1))))
                    apart(sp)
                if n >= B and c == 0 and n % 2 == 0:
                    sp.wait_ge(maskop_done, st.at(lambda s: (s + ahead - B) // 2 + 1))
                    apart(sp)
                for row, part in ((0, khi), (PR, klo), (2 * PR, khi)):
                    sp.dma_start(kop[row:row + PR, dst, :, cols], part[:, cols]).then_inc(kop_in[c], 16)
                if n >= B:
                    half = S * (n % 2)
                    sp.dma_start(kop[MASK0:SHIFT0, dst, :, cols],
                                 maskop[half:half + S, cols].unsqueeze(1).broadcast_to([S, PAIRS, CW])
                                 ).then_inc(kop_in[c], 16)

            def step(st):
                s = st.s
                if has_m(s - 1):
                    sp.wait_ge(fy_free, st.at(lambda s: upto(fy_uses, s, "ct", True)))
                    apart(sp)
                    sp.dma_start(qexp[SHIFT0:ROWS, (s - 1) % 2, :, :, :].rearrange("r p j q -> r (p j q)"),
                                 ct[:, :]).then_inc(shift_in, 16)
                if has_k(s - 1):
                    key_chunk(st, 0, 2)
                if has_m(s):
                    if s == 0:
                        sp.wait_ge(init_dma, 128)
                    sp.wait_ge(qmax_in, st.at(lambda s: 96 * (s + 1)))
                    apart(sp)
                    if is_batch(s - 2):
                        sp.wait_ge(st_ready, st.at(lambda s: 2 * KT * (s - 1)))
                        apart(sp)
                    sp.dma_start(qexp[0:SHIFT0, s % 2, :, :, :], qmax[0:SHIFT0, s % 2, :, :, :]).then_inc(qexp_in[s % 2], 16)
                if s == 0:
                    late_loads()
                if has_k(s):
                    key_chunk(st, 1, 0)
                    if has_q(s):
                        sp.wait_ge(fh_free, st.at(lambda s: upto(fh_uses, s, "q", True)))
                        apart(sp)
                    if s >= 1:
                        sp.wait_ge(mx_ready, st.at(lambda s: NMAX * s))
                        apart(sp)
                        sp.wait_ge(qexp_in[(s - 1) % 2], st.at(lambda s: 16 * ((s - 1) // 2 + 1)))
                        apart(sp)
                    half = S * ((s + 1) % 2)
                    for row, part in ((0, qhi), (PR, qhi), (2 * PR, qlo)):
                        for j in range(2):
                            sp.dma_start(qmax[row + HD * j:row + HD * (j + 1), (s + 1) % 2, :, j, :],
                                         part[64 * j:64 * (j + 1), half:half + S]).then_inc(qmax_in, 16)
                if s >= B - 1 and has_mask(s + 1):
                    group = st.at(lambda s: (s + 3 - B) // 2)
                    sp.wait_ge(mask_done, st.at(maskraw_count))
                    apart(sp)
                    src = mask[group] if isinstance(group, int) else mask[bass.ds(group, 1)].rearrange("a t k -> (a t) k")
                    sp.dma_start(maskin[:, :], src).then_inc(mask_in, 16)
                if has_k(s):
                    key_chunk(st, 1, 1)
                if 0 <= s <= NB - 3:
                    sp.wait_ge(kv_ready, st.at(lambda s: upto(kv_uses, s, "v2")))
                    apart(sp)
                    if st.turn is None:
                        src = ctxT[(s + 2) % B]
                    else:
                        src = ctxT[bass.ds(st.at(lambda s: s + 2 - (B if st.s >= B else 0)) & (B - 1), 1)].rearrange("a d k -> (a d) k")
                    sp.dma_start(C[:, s % 2, :], src).then_inc(c_in[s % 2], 16)

            run_steps(sp, step)
            sp.wait_ge(x_done, 2 * G)
            sp.dma_start(out.rearrange("(g t) d -> t g d", g=G),
                         X[:, :].rearrange("t (g d) -> t g d", g=G)).then_inc(stored, 16)
            sp.wait_ge(stored, 16)

        @block.gpsimd
        def _(pool):
            nc.gpsimd.memset(shift_rows[:, 0, :], -BIG).then_inc(init_p, 1)
            nc.gpsimd.memset(shift_rows[:, 1, :], -1.0).then_inc(init_p, 1)
            nc.gpsimd.memset(maskop[:, :], 0.0).then_inc(init_p, 1)
            nc.gpsimd.memset(pick[:, :, :], 0.0).then_inc(init_p, 1)
            pool.wait_ge(init_p, 4)
            nc.gpsimd.affine_select(out=pick[:, :, :], in_=pick[:, :, :], compare_op=ALU.not_equal, fill=BIG,
                                    base=0, pattern=[[0, H], [-1, S]], channel_multiplier=1).then_inc(init_p, 1)
            nc.gpsimd.memset(ident[:, :], 0.0).then_inc(init_p, 1)
            nc.gpsimd.memset(ident16[:, :], 0.0).then_inc(init_p, 1)
            nc.gpsimd.memset(sel[:, :], 0.0).then_inc(init_p, 1)
            nc.gpsimd.memset(before_me[:, :, :], 1.0).then_inc(init_p, 1)
            nc.gpsimd.memset(mhalf[:, :], -0.5).then_inc(init_p, 1)
            nc.gpsimd.memset(keep[:, :], 1.0).then_inc(init_p, 1)
            pool.wait_ge(init_p, 11)
            for m in (ident, ident16):
                nc.gpsimd.affine_select(out=m[:, :], in_=m[:, :], compare_op=ALU.not_equal, fill=1.0,
                                        base=0, pattern=[[-1, 128]], channel_multiplier=1).then_inc(init_p, 1)
            nc.gpsimd.affine_select(out=sel[:, :].rearrange("p (g i) -> p g i", g=4),
                                    in_=sel[:, :].rearrange("p (g i) -> p g i", g=4),
                                    compare_op=ALU.not_equal, fill=1.0, base=-PR,
                                    pattern=[[-32, 4], [0, 32]], channel_multiplier=1).then_inc(init_p, 1)
            nc.gpsimd.affine_select(out=before_me[:, :, :], in_=before_me[:, :, :], compare_op=ALU.is_gt, fill=0.0,
                                    base=0, pattern=[[1, NE], [-1, NE]], channel_multiplier=0).then_inc(init_p, 1)
            linked = [0]

            def link(ins):
                linked[0] += 1
                ins.then_inc(pool_link, 1)

            def pool_links(s):
                return sum(2 * has_q(t) + is_batch(t - 2) + has_a(t) for t in range(-1, s))

            def step(st):
                s = st.s
                if has_mask(s):
                    pool.wait_ge(mask_in, st.at(lambda s: 16 * (maskraw_count(s) + 1)))
                    apart(pool)
                    nc.gpsimd.tensor_scalar(maskraw[:, :], maskin[:, :], 0, -BIG, ALU.is_equal, ALU.mult
                                            ).then_inc(mask_done, 1)
                if has_q(s):
                    pool.wait_ge(statq_done, st.at(lambda s: q_count(s) + 1))
                    apart(pool)
                    nc.gpsimd.tensor_scalar(veq[:, :], mvq[:, 1:2], EPS, None, ALU.add).then_inc(pool_link, 1)
                    pool.wait_ge(pool_link, st.at(lambda s: pool_links(s) + 1))
                    nc.gpsimd.tensor_tensor(rsq[:, :], veq[:, :], mhalf[:, :], ALU.pow).then_inc(pool_link, 1)
                    pool.wait_ge(pool_link, st.at(lambda s: pool_links(s) + 2))
                    if s + 1 >= B:
                        pool.wait_ge(keep_done, st.at(lambda s: mask_count(s) + 1))
                    nc.gpsimd.tensor_tensor(rkq[:, :], rsq[:, :], keep[:, :], ALU.mult).then_inc(rstdq_done, 1)
                if has_q(s) and s + 1 >= B:
                    for c in range(CH):
                        pool.wait_ge(kop_in[c], st.at(b_total))
                        apart(pool)
                    nc.gpsimd.tensor_copy(maskop[:, :], maskraw[:, :]).then_inc(maskop_done, 1)
                if is_batch(s - 2):
                    l, n = layer_of(s - 2), 2 * has_q(s) + 1
                    pool.wait_ge(fy_free, st.at(lambda s: upto(fy_uses, s, "sum", True)))
                    apart(pool)
                    if s >= 4:
                        pool.wait_ge(fy_ready, st.at(lambda s: upto(fy_uses, s - 2 + (s + 1) % 2, "y")))
                        apart(pool)
                    nc.gpsimd.tensor_tensor(ON0[:, :], OM[:, s % 2, :], rden[:, :], ALU.mult).then_inc(pool_link, 1)
                    pool.wait_ge(pool_link, st.at(lambda s: pool_links(s) + n))
                    nc.gpsimd.tensor_tensor(ON[:, :, :, s % 2, :].rearrange("p r j q -> p (r j) q"),
                                            ON0[:, :].rearrange("p (n q) -> p n q", q=S),
                                            bvm[:, l, :, :, :].rearrange("p r j q -> p (r j) q"),
                                            ALU.add).then_inc(on_done, 1)
                if has_a(s):
                    n = 2 * has_q(s) + 2
                    pool.wait_ge(statf_done, st.at(lambda s: a_count(s) + 1))
                    apart(pool)
                    nc.gpsimd.tensor_scalar(vef[:, :], mvf[:, 1:2], EPS, None, ALU.add).then_inc(pool_link, 1)
                    pool.wait_ge(pool_link, st.at(lambda s: pool_links(s) + n))
                    nc.gpsimd.tensor_tensor(rsf[:, :], vef[:, :], mhalf[:, :], ALU.pow).then_inc(rstdf_done, 1)

            run_steps(pool, step)

        @block.scalar
        def _(act):
            act.wait_ge(w_in, 48)
            nc.scalar.activation(gains[:, :], bc[:, GX:GX + 4], ACT.Tanh).then_inc(init_a, 1)
            act.wait_ge(init_v, 7)

            def exps(st, kt, h):
                back, tile = tile_at(kt, E_LAG)
                if not is_batch(st.s - back):
                    return
                slot = tile % RING
                act.wait_ge(st_ready, st.at(lambda s: 2 * (KT * (s - back) + tile) + h + 1))
                if h == 0 and (st.s > back or tile >= RING):
                    act.wait_ge(av_done, st.at(lambda s: KT * (s - back) + tile - RING + 1))
                nc.scalar.activation(P[0:KP, slot, h * 4 * T:(h + 1) * 4 * T], pST[0:KP, h, 0:4 * T], ACT.Exp,
                                     scale=EXP_SCALE).then_inc(exp_done, 1)

            def step(st):
                s = st.s
                for kt in range(KT):
                    exps(st, kt, 0)
                    for use in [u[1] for u in kv_uses(s) if u[0] == kt]:
                        c = int(use[1])
                        act.wait_ge(kv_ready, st.at(lambda s: upto(kv_uses, s, use)))
                        if use[0] == "k":
                            if s >= 0:
                                act.wait_ge(kop_in[c], st.at(b_total))
                            nc.scalar.activation(khi[:, c * CW:(c + 1) * CW], pKV[:, 0:CW], ACT.Identity,
                                                 bias=w(f"bk{layer_of(s + 1)}"), scale=1.0).then_inc(khi_done, 1)
                        else:
                            if s >= 2:
                                act.wait_ge(av_done, st.at(lambda s: KT * (s - 1)))
                            nc.scalar.activation(
                                V[0:KP, s % 2, 4 * c:4 * c + 4, :, 0:PR].rearrange("k t p i -> k (t p) i"),
                                pKV[0:KP, :].rearrange("k (m i) -> k m i", i=PR), ACT.Copy).then_inc(kv_free, 1)
                    exps(st, kt, 1)
                    if kt == 0 and has_q(s) and s + 1 >= B:
                        act.wait_ge(mask_done, st.at(lambda s: mask_count(s) + 1))
                        nc.scalar.activation(masksink[:, :], maskraw[:, :], ACT.Copy, accum_out=masksum[:, :]
                                             ).then_inc(masksum_done, 1)
                    if kt == 11 and has_a(s):
                        act.wait_ge(logit_done, st.at(lambda s: a_count(s) + 1))
                        if layer_of(s - 2) == 0:
                            nc.scalar.activation(ge[:, :], lg[:, :], ACT.Exp, bias=lneg[:, :], scale=1.0,
                                                 accum_out=gse[:, :]).then_inc(gexp_done, 1)
                        else:
                            nc.scalar.activation(ge[:, :], lg[:, :], ACT.Exp, scale=-1.0).then_inc(gexp_done, 1)
                    if kt == 7 and has_f(s):
                        act.wait_ge(fh_free, st.at(lambda s: before(fh_uses, s + 1, True)))
                        if layer_of(s - 3) == 0:
                            nc.scalar.activation(HR[:, :, :], HR[:, :, :], ACT.Gelu).then_inc(gelu_done, 2)
                        else:
                            nc.scalar.activation(HR[:, 0:4, :], HR[:, 0:4, :], ACT.Gelu).then_inc(gelu_done, 1)
                            nc.scalar.activation(HR[0:F1, 4, :], HR[0:F1, 4, :], ACT.Gelu).then_inc(gelu_done, 1)

            run_steps(act, step)

        @block.vector
        def _(dve):
            nc.vector.memset(qmax[:, :, :, :, :].rearrange("p b r j q -> p (b r j q)"), 0.0).then_inc(init_v, 1)
            dve.wait_ge(w_in, 48)
            for l in range(LAYERS):
                a = COLS[f"wq{l}"][0]
                nc.vector.tensor_scalar(W[:, a:a + 2 * D], W[:, a:a + 2 * D], QK_SCALE, None, ALU.mult).then_inc(init_v, 1)
            a = COLS["bk0"][0]
            nc.vector.tensor_scalar(W[:, a:a + 2], W[:, a:a + 2], QK_SCALE, None, ALU.mult).then_inc(init_v, 1)
            nc.vector.tensor_scalar(bq_row[:, :], bq_row[:, :], QK_SCALE, None, ALU.mult).then_inc(init_v, 1)
            Vf = V[:, :, :, :, :].rearrange("k b t p i -> k (b t p) i")
            nc.vector.memset(Vf[:, :, PR:PR + 1], 1.0).then_inc(init_v, 1)
            nc.vector.memset(Vf[:, :, PR + 1:32], 0.0).then_inc(init_v, 1)
            nc.vector.memset(woE[:, :, :, :], 0.0).then_inc(init_w, 1)
            nc.vector.memset(bvE[:, :, :], 0.0).then_inc(init_w, 1)
            nc.vector.memset(b2x[:, 0, :], 0.0).then_inc(init_w, 1)
            dve.wait_ge(init_p, 15)
            dve.wait_ge(x_in, 16)

            def late_constants():
                nc.vector.memset(ones[:, :], 1.0).then_inc(init_l, 1)
                nc.vector.memset(gate[:, NE:NE + 1], 1.0).then_inc(init_l, 1)
                ig = ident[:, :].rearrange("p (g i) -> p g i", g=4)
                for k, (a, b) in enumerate(((0, HD), (HD, PR), (PR, PR + 1))):
                    nc.vector.tensor_reduce(rowmask[:, k:k + 1], ig[:, :, a:b], AX.XY, ALU.add).then_inc(init_l, 1)
                dve.wait_ge(init_l, 5)
                dve.wait_ge(wo_in, 16 * 16)
                dve.wait_ge(init_a, 1)
                for j in range(2):
                    for l in range(LAYERS):
                        for r in range(2):
                            nc.vector.tensor_scalar(bvm[:, l, r, j, :], ones[:, 0:S], rowmask[:, j:j + 1],
                                                    bvE[:, l, r:r + 1], ALU.mult, ALU.mult).then_inc(init_l, 1)
                    nc.vector.tensor_scalar(headmask[:, :, j, :], ones[:, :].rearrange("p (r q) -> p r q", r=2),
                                            rowmask[:, j:j + 1], rowmask[:, 2:3], ALU.mult, ALU.add).then_inc(init_l, 1)
                for l in range(LAYERS):
                    nc.vector.tensor_scalar(tbo[:, l, :], bc[0:T, BO + l * D:BO + (l + 1) * D], gains[0:T, l:l + 1], None,
                                            ALU.mult).then_inc(init_l, 1)
                dve.wait_ge(init_l, 17)
                dve.wait_ge(f_in, 16 * 8)

            def links_before(s):
                return sum(links(t) for t in range(-1, s))

            def step(st):
                s = st.s
                linked = [0]

                def link(ins, alone=False):
                    linked[0] += 1
                    k = linked[0]
                    ins.then_inc(dve_link, 1)
                    dve.wait_ge(dve_link, st.at(lambda s: links_before(s) + k))
                    if alone:
                        apart(dve)

                def xg(f):
                    v = st.at(lambda s: D * (f(s) % G))
                    return X[:, bass.ds(v, D)] if st.turn is not None else X[:, v:v + D]

                def ready(sem_, uses, back, name):
                    dve.wait_ge(sem_, st.at(lambda s: upto(uses, s - back, name)))

                def freed(sem_, uses, back, name):
                    dve.wait_ge(sem_, st.at(lambda s: upto(uses, s - back, name, True)))

                def low_parts(back, use):
                    c, n = int(use[1]), s - back + 1
                    dve.wait_ge(khi_done, st.at(lambda s: CH * (s - back + 1) + c + 1))
                    nc.vector.scalar_tensor_tensor(
                        out=klo[:, c * CW:(c + 1) * CW], in0=pKV[:, 0:CW], scalar=w(f"bk{layer_of(n)}"),
                        in1=khi[:, c * CW:(c + 1) * CW], op0=ALU.add, op1=ALU.subtract).then_inc(kv_free, 1)

                def hidden(back, use):
                    e, t = int(use[1]), s - back
                    ready(fh_ready, fh_uses, back, use)
                    if layer_of(t - 2 if has_a(t) else t - 3) == 0:
                        nc.vector.tensor_tensor(
                            HR[:, F0C * e:F0C * (e + 1), :], pFH[:, 0:F0C * T].rearrange("p (c t) -> p c t", c=F0C),
                            w("b1_0")[:, F0C * e:F0C * (e + 1)].unsqueeze(2).broadcast_to([128, F0C, T]),
                            ALU.add).then_inc(fh_free, 1)
                    elif e == 0:
                        nc.vector.tensor_tensor(
                            HR[:, 0:4, :], pFH[:, 0:4 * T].rearrange("p (c t) -> p c t", c=4),
                            w("b1_1").unsqueeze(2).broadcast_to([128, 4, T]), ALU.add).then_inc(fh_free, 1)
                    else:
                        nc.vector.tensor_scalar(HR[0:F1, 4, :], pFH[0:F1, 0:T], bs1b[:, 0:1], None, ALU.add
                                                ).then_inc(fh_free, 1)

                def from_fh(back, use):
                    if use == "qT":
                        ready(fh_ready, fh_uses, back, use)
                        nc.vector.tensor_copy(xnqT[:, :], pFH[:, 0:T]).then_inc(fh_free, 1)
                        nc.vector.tensor_copy(keepT[:, :], pFH[0:1, 128:128 + T]).then_inc(fh_free, 1)
                    elif use == "q":
                        ready(fh_ready, fh_uses, back, use)
                        if s > 0:
                            dve.wait_ge(qmax_in, st.at(lambda s: 96 * (s + 1)))
                        link(nc.vector.tensor_copy(qhi[:, :], pFH[:, 0:T]))
                        nc.vector.tensor_tensor(qlo[:, :], pFH[:, 0:T], qhi[:, :], ALU.subtract).then_inc(fh_free, 1)
                    else:
                        hidden(back, use)

                def from_fy(back, use):
                    ready(fy_ready, fy_uses, back, use)
                    l = layer_of(s - back - 2)
                    if use == "ct":
                        if s > 1:
                            dve.wait_ge(shift_in, st.at(lambda s: 16 * (s - 1)))
                        nc.vector.tensor_copy(ct[:, :], pFY[0:2 * PAIRS, 0:T // 2].bitcast(F16)).then_inc(fy_free, 1)
                    elif use == "sum":
                        if s > 2:
                            dve.wait_ge(on_done, st.at(lambda s: s - 2))
                        nc.vector.reciprocal(rden[:, :], pFY[:, 0:2 * T]).then_inc(fy_free, 1)
                    elif use == "y":
                        nc.vector.scalar_tensor_tensor(out=XF0[:, :], in0=pFY[0:T, 0:D], scalar=gains[0:T, l:l + 1],
                                                       in1=xg(lambda s: (s - 3) // 2), op0=ALU.mult, op1=ALU.add
                                                       ).then_inc(fy_free, 1)
                        freed(fy_free, fy_uses, back, use)
                        link(nc.vector.tensor_tensor(XF[:, :], XF0[:, :], tbo[:, l, :], ALU.add))
                        link(nc.vector.bn_stats(stf[:, :], XF[:, :]), alone=True)
                        nc.vector.bn_aggr(mvf[:, :], stf[:, :]).then_inc(statf_done, 1)
                    elif use == "xT":
                        nc.vector.tensor_copy(xnfT[:, :], pFY[:, 0:T]).then_inc(fy_free, 1)
                    elif use == "lg":
                        nc.vector.tensor_copy(lg[:, :], pFY[0:T, 0:NE]).then_inc(fy_free, 1)
                        freed(fy_free, fy_uses, back, use)
                        if l == 0:
                            link(nc.vector.tensor_reduce(lmax[:, :], lg[:, :], AX.X, ALU.max))
                        nc.vector.tensor_scalar(lneg[:, :], lmax[:, :] if l == 0 else lg[:, 0:1], -1.0, None,
                                                ALU.mult).then_inc(logit_done, 1)
                    elif use == "gT":
                        nc.vector.tensor_copy(gateT[:, :], pFY[0:NE + 1, 0:T]).then_inc(fy_free, 1)
                    elif use == "yb":
                        l = layer_of(s - 4)
                        nc.vector.tensor_tensor(acc[:, 0, :], pFY[0:T, 0:D], acc[:, 1, :], ALU.add).then_inc(fy_free, 1)
                        freed(fy_free, fy_uses, back, use)
                        nc.vector.scalar_tensor_tensor(out=xg(lambda s: (s - 5) // 2), in0=acc[:, 0, :],
                                                       scalar=gains[0:T, 2 + l:3 + l], in1=XF[:, :],
                                                       op0=ALU.mult, op1=ALU.add).then_inc(x_done, 1)
                    else:
                        for j, e in enumerate(experts_of(int(use[1]))):
                            y = pFY[0:T, j * D:(j + 1) * D]
                            if e == 0:
                                ins = nc.vector.tensor_scalar(acc[:, 0, :], y, gate[:, 0:1], None, ALU.mult)
                            else:
                                ins = nc.vector.scalar_tensor_tensor(out=acc[:, j, :], in0=y, scalar=gate[:, e:e + 1],
                                                                     in1=acc[:, 1 - j, :], op0=ALU.mult, op1=ALU.add)
                            if j:
                                ins.then_inc(fy_free, 1)
                                freed(fy_free, fy_uses, back, use)
                            else:
                                link(ins)

                def shares(kt):
                    pj = gp[:, :].unsqueeze(1).broadcast_to([T, NE, NE])
                    pe_ = gp[:, :].unsqueeze(2).broadcast_to([T, NE, NE])
                    if kt == 1:
                        dve.wait_ge(gexp_done, st.at(lambda s: a_count(s)))
                        if layer_of(s - 3) == 0:
                            link(nc.vector.reciprocal(g1[:, 0:1], gse[:, :]))
                            link(nc.vector.tensor_scalar(gp[:, :], ge[:, :], g1[:, 0:1], None, ALU.mult))
                        else:
                            link(nc.vector.tensor_scalar(g1[:, :], ge[:, :], 1.0, None, ALU.add))
                            link(nc.vector.reciprocal(g2[:, :], g1[:, :]))
                            link(nc.vector.tensor_scalar(gp[:, :], g2[:, :], bc[0:T, RS:RS + 1], None, ALU.mult))
                    if kt == 2:
                        nc.vector.tensor_tensor(ggt[:, :, :], pj, pe_, ALU.is_gt)
                        link(nc.vector.tensor_tensor(geq[:, :, :], pj, pe_, ALU.is_equal))
                        link(nc.vector.tensor_tensor(gel[:, :, :], geq[:, :, :], before_me[:, :, :], ALU.mult))
                    if kt == 3:
                        link(nc.vector.tensor_tensor(grk[:, :, :], gel[:, :, :], ggt[:, :, :], ALU.add))
                        link(nc.vector.tensor_reduce(rank[:, :], grk[:, :, :], AX.X, ALU.add))
                    if kt == 4:
                        link(nc.vector.scalar_tensor_tensor(out=gsp[:, :], in0=rank[:, :], scalar=1.5, in1=gp[:, :],
                                                            op0=ALU.is_lt, op1=ALU.mult))
                        link(nc.vector.tensor_reduce(gden[:, :], gsp[:, :], AX.X, ALU.add))
                    if kt == 5:
                        link(nc.vector.reciprocal(grd[:, :], gden[:, :]))
                        nc.vector.tensor_scalar(gate[:, 0:NE], gsp[:, :], grd[:, :], None, ALU.mult).then_inc(gate_done, 1)

                if s == 1:
                    late_constants()
                for kt in range(KT):
                    if kt == 0 and has_m(s - 1):
                        dve.wait_ge(max_done, st.at(lambda s: NMAX * s))
                        link(nc.vector.tensor_reduce(m8[:, :], mx[:, (s - 1) % 2, :, :].rearrange("t c p -> t p c"), AX.X, ALU.max))
                        if s > 1:
                            dve.wait_ge(fy_ready, st.at(lambda s: upto(fy_uses, s - 1, "ct")))
                        link(nc.vector.tensor_scalar(cc[:, 0, :], m8[:, :], 1.0 / BIG, None, ALU.mult))
                        nc.vector.scalar_tensor_tensor(out=cc[:, 1, :], in0=cc[:, 0, :], scalar=-BIG, in1=m8[:, :],
                                                       op0=ALU.mult, op1=ALU.add).then_inc(cc_ready, 1)
                    for back, use in issued_before(fy_uses, s, kt):
                        from_fy(back, use)
                    for back, use in issued_before(fh_uses, s, kt):
                        from_fh(back, use)
                    if kt == AV_LAG and is_batch(s - 2):
                        dve.wait_ge(av_done, st.at(lambda s: KT * (s - 1)))
                        if s >= 4:
                            dve.wait_ge(on_done, st.at(lambda s: s - 3))
                        nc.vector.tensor_tensor(OM[:, s % 2, :], pO[:, 0:2 * T],
                                                headmask[:, :, :, :].rearrange("p r j q -> p (r j q)"),
                                                ALU.mult).then_inc(o_free, 1)
                    if has_m(s):
                        m = MAXES_PER_KT * kt
                        dve.wait_ge(mx_ready, st.at(lambda s: NMAX * s + m + 1))
                        nc.vector.tensor_reduce(mx[:, s % 2, m // PAIRS, m % PAIRS:m % PAIRS + 1],
                                                pMX[0:T, 0, 0:CW], AX.X, ALU.max).then_inc(max_done, 1)
                    if has_a(s) and kt == 9:
                        dve.wait_ge(rstdf_done, st.at(lambda s: a_count(s) + 1))
                        nc.vector.tensor_scalar(xnf[:, :], XF[:, :], mvf[:, 0:1], rsf[:, :],
                                                ALU.subtract, ALU.mult).then_inc(xnf_done, 1)
                    for back, use in issued_before(kv_uses, s, kt):
                        if use[0] == "k":
                            low_parts(back, use)
                    if has_m(s):
                        m = MAXES_PER_KT * kt + 1
                        dve.wait_ge(mx_ready, st.at(lambda s: NMAX * s + m + 1))
                        nc.vector.tensor_reduce(mx[:, s % 2, m // PAIRS, m % PAIRS:m % PAIRS + 1],
                                                pMX[0:T, 1, 0:CW], AX.X, ALU.max).then_inc(max_done, 1)
                    if has_f(s):
                        shares(kt)
                    if has_q(s) and kt == 1:
                        if s + 1 >= B:
                            dve.wait_ge(x_done, st.at(lambda s: (s + 1 - B) // 2 + 1))
                        link(nc.vector.bn_stats(stq[:, :], xg(lambda s: (s + 1) // 2)), alone=True)
                        nc.vector.bn_aggr(mvq[:, :], stq[:, :]).then_inc(statq_done, 1)
                    if has_q(s) and s + 1 >= B and kt == 2:
                        dve.wait_ge(masksum_done, st.at(lambda s: mask_count(s) + 1))
                        nc.vector.tensor_scalar(keep[:, :], masksum[:, :], -BIG * (S2 - 0.5), None, ALU.is_gt
                                                ).then_inc(keep_done, 1)
                    if has_q(s) and kt == 3:
                        dve.wait_ge(rstdq_done, st.at(lambda s: q_count(s) + 1))
                        nc.vector.tensor_scalar(xnq[:, :], xg(lambda s: (s + 1) // 2), mvq[:, 0:1], rkq[:, :],
                                                ALU.subtract, ALU.mult).then_inc(xnq_done, 1)
                assert linked[0] == links(s), (s, linked[0], links(s))

            run_steps(dve, step)

        @block.tensor
        def _(pe):
            pe.wait_ge(init_v, 5)
            pe.wait_ge(init_p, 15)

            def score_half(st, kt, h):
                back, tile = tile_at(kt, E_LAG)
                if not is_batch(st.s - back):
                    return
                b = (st.s - back) % 2
                if tile == 0 and h == 0:
                    pe.wait_ge(qexp_in[b], st.at(lambda s: 16 * ((s - back) // 2 + 1)))
                    pe.wait_ge(shift_in, st.at(lambda s: 16 * (s - back + 1)))
                if st.s > back or tile > 0:
                    pe.wait_ge(exp_done, st.at(lambda s: 2 * (KT * (s - back) + tile) + h - 1))
                for i in range(4):
                    p = 4 * h + i
                    mm = nc.tensor.matmul(pST[0:KP, h, i * T:(i + 1) * T],
                                          kop[0:ROWS, b, p, tile * KP:(tile + 1) * KP],
                                          qexp[0:ROWS, b, p, :, :].rearrange("r j q -> r (j q)"),
                                          start=True, stop=True)
                mm.then_inc(st_ready, 1)

            def weigh(st, kt):
                back, tile = tile_at(kt, AV_LAG)
                if not is_batch(st.s - back):
                    return
                b = (st.s - back) % 2
                if tile == 0:
                    pe.wait_ge(kv_free, st.at(lambda s: upto(kv_uses, s - back, "v2", True)))
                    if st.s > back:
                        pe.wait_ge(o_free, st.at(lambda s: s - back))
                for r in range(2):
                    pe.wait_ge(exp_done, st.at(lambda s: 2 * (KT * (s - back) + tile) + r + 1))
                    for g in range(4):
                        p = 4 * r + g
                        mm = nc.tensor.matmul(pO[32 * g:32 * (g + 1), r * T:(r + 1) * T],
                                              V[0:KP, b, tile, p, :], P[0:KP, tile % RING, p * T:(p + 1) * T],
                                              start=(tile == 0 and r == 0), stop=(tile == KT - 1), skip_group_check=True)
                mm.then_inc(av_done, 1)

            def max_scores(st, m):
                c, p = divmod(m, PAIRS)
                if m == 0:
                    pe.wait_ge(qmax_in, st.at(lambda s: 96 * (s + 1)))
                    if st.s == 0:
                        pe.wait_ge(init_dma, 128)
                if p == 0:
                    pe.wait_ge(kop_in[c], st.at(b_total))
                if st.s > 0 or m > 1:
                    pe.wait_ge(max_done, st.at(lambda s: NMAX * s + m - 1))
                nc.tensor.matmul(pMX[0:T, m % 2, 0:CW],
                                 qmax[0:SHIFT0, st.s % 2, p, :, :].rearrange("r j q -> r (j q)"),
                                 kop[0:SHIFT0, st.s % 2, p, c * CW:(c + 1) * CW], start=True, stop=True
                                 ).then_inc(mx_ready, 1)

            def step(st):
                s = st.s
                if s == 3:
                    pe.wait_ge(init_l, 17)
                    pe.wait_ge(f_in, 16 * 8)

                def free(sem_, uses, name):
                    first = before(uses, s) == 0 and uses(s)[0][1] == name
                    if not first:
                        def n(s):
                            u = [x for x in uses(s) if x[1] == name][0]
                            return upto(uses, s, name, True) - u[2]
                        pe.wait_ge(sem_, st.at(n))

                for kt in range(KT):
                    if has_m(s):
                        max_scores(st, MAXES_PER_KT * kt)
                    if kt != AV_LAG:
                        weigh(st, kt)
                    score_half(st, kt, 0)
                    for use in [u[1] for u in kv_uses(s) if u[0] == kt]:
                        c = int(use[1])
                        free(kv_free, kv_uses, use)
                        if use[0] == "k":
                            if c == 0:
                                pe.wait_ge(c_in[(s + 1) % 2], st.at(lambda s: 16 * ((s + 1) // 2 + 1)))
                            nc.tensor.matmul(pKV[:, 0:CW], w(f"wk{layer_of(s + 1)}"),
                                             C[:, (s + 1) % 2, c * CW:(c + 1) * CW], start=True, stop=True
                                             ).then_inc(kv_ready, 1)
                        else:
                            for i in range(4):
                                t = 4 * c + i
                                mm = nc.tensor.matmul(pKV[0:KP, i * D:(i + 1) * D], C[:, s % 2, t * KP:(t + 1) * KP],
                                                      w(f"wv{layer_of(s)}"), start=True, stop=True)
                            mm.then_inc(kv_ready, 1)
                    if has_m(s):
                        max_scores(st, MAXES_PER_KT * kt + 1)
                    score_half(st, kt, 1)

                    for use in [u[1] for u in fy_uses(s) if u[0] == kt]:
                        free(fy_free, fy_uses, use)
                        if use == "sum":
                            pe.wait_ge(o_free, st.at(lambda s: s - 1))
                            mm = nc.tensor.matmul(pFY[:, 0:2 * T], sel[:, :], OM[:, s % 2, :], start=True, stop=True)
                        elif use == "y":
                            pe.wait_ge(on_done, st.at(lambda s: s - 1))
                            l = layer_of(s - 2)
                            for r in range(2):
                                for j in range(2):
                                    mm = nc.tensor.matmul(pFY[0:T, 0:D], ON[:, r, j, :, :].rearrange("p b q -> p (b q)"), woE[:, l, r, :],
                                                          start=(r == 0 and j == 0), stop=(r == 1 and j == 1))
                        elif use == "xT":
                            pe.wait_ge(xnf_done, st.at(lambda s: a_count(s) + 1))
                            mm = nc.tensor.transpose(pFY[:, 0:T], xnf[:, :], ident[0:T, 0:T])
                        elif use == "lg":
                            mm = nc.tensor.matmul(pFY[0:T, 0:NE], xnfT[:, :], w(f"gate{layer_of(s - 2)}"),
                                                  start=True, stop=True)
                        elif use == "gT":
                            pe.wait_ge(gate_done, st.at(lambda s: f_count(s) + 1))
                            mm = nc.tensor.transpose(pFY[0:NE + 1, 0:T], gate[:, :], ident[0:T, 0:T])
                        elif use == "ct":
                            pe.wait_ge(cc_ready, st.at(lambda s: s))
                            mm = nc.tensor.transpose(pFY[0:2 * PAIRS, 0:T // 2].bitcast(F16),
                                                     cc[:, :, :].rearrange("t i p -> t (i p)"), ident16[0:T, 0:T])
                        elif use == "yb":
                            l = layer_of(s - 4)
                            if l == 1:
                                nc.tensor.matmul(pFY[0:T, 0:D], HR[0:F1, 4, :], ws2b[:, :], start=True, stop=False)
                            mm = nc.tensor.matmul(pFY[0:T, 0:D], gateT[:, :], b2x[:, l, :], start=(l == 0), stop=True)
                        else:
                            if use == "y0":
                                pe.wait_ge(gelu_done, st.at(lambda s: 2 * (f_count(s) + 1)))
                            l = layer_of(s - 4 if s % 2 else s - 3)
                            i = int(use[1])
                            for j, e in enumerate(experts_of(i)):
                                o = pFY[0:T, j * D:(j + 1) * D]
                                if l == 0:
                                    for c in range(F0C):
                                        mm = nc.tensor.matmul(o, HR[:, F0C * e + c, :], w2a[:, e, c, :],
                                                              start=(c == 0), stop=(c == F0C - 1))
                                else:
                                    half = slice(F1 * (e % 2), F1 * (e % 2 + 1))
                                    mm = nc.tensor.matmul(o, HR[half, e // 2, :], w2b[half, e // 2, :],
                                                          start=True, stop=True)
                        mm.then_inc(fy_ready, 1)

                    if kt == AV_LAG:
                        weigh(st, kt)
                    for use in [u[1] for u in fh_uses(s) if u[0] == kt]:
                        free(fh_free, fh_uses, use)
                        if use == "qT":
                            pe.wait_ge(xnq_done, st.at(lambda s: q_count(s) + 1))
                            nc.tensor.transpose(pFH[:, 0:T], xnq[:, :], ident[0:T, 0:T])
                            nc.tensor.transpose(pFH[0:1, 128:128 + T], keep[:, :], ident[0:T, 0:T]).then_inc(fh_ready, 1)
                        elif use == "q":
                            l = layer_of(s + 1)
                            nc.tensor.matmul(pFH[:, 0:T], w(f"wq{l}"), xnqT[:, :], start=True, stop=False)
                            nc.tensor.matmul(pFH[:, 0:T], bq_row[:, l * D:(l + 1) * D], keepT[:, :],
                                             start=False, stop=True).then_inc(fh_ready, 1)
                        else:
                            e = int(use[1:])
                            l = layer_of(s - 2 if s % 2 else s - 3)
                            if l == 0:
                                for c in range(F0C):
                                    mm = nc.tensor.matmul(pFH[:, c * T:(c + 1) * T], w1a[:, e, c * 128:(c + 1) * 128],
                                                          xnfT[:, :], start=True, stop=True)
                            elif e == 0:
                                for c in range(4):
                                    mm = nc.tensor.matmul(
                                        pFH[:, c * T:(c + 1) * T],
                                        w1b[:, 2 * c:2 * c + 2, :].rearrange("d e f -> d (e f)"),
                                        xnfT[:, :], start=True, stop=True)
                            else:
                                mm = nc.tensor.matmul(pFH[0:F1, 0:T], w("ws1"), xnfT[:, :], start=True, stop=True)
                            mm.then_inc(fh_ready, 1)

            run_steps(pe, step)


def kernel(**inputs):
    import numpy as np
    import concourse.bacc as bacc
    from concourse.bass_utils import run_bass_kernel_spmd

    def arr(name):
        return np.asarray(inputs[name])

    def pairs_last(a):
        return a.reshape(a.shape[:-1] + (PAIRS, PR)).swapaxes(-1, -2).reshape(a.shape)

    x0 = arr("x")
    wq = [arr("L0_xattn_Wq").T, arr("L1_xattn_wq_kernel")]
    wk = [arr("L0_xattn_Wk").T, arr("L1_xattn_wk_kernel")]
    wv = [arr("L0_xattn_Wv").T, arr("L1_xattn_wv_kernel")]
    parts = {"bk0": pairs_last(arr("L0_xattn_bk"))[:, None], "bk1": pairs_last(arr("L1_xattn_wk_bias"))[:, None],
             "gate0": arr("L0_ffn_gate_w"), "gate1": arr("L1_ffn_gate_W"),
             "b1_0": arr("L0_ffn_b1").reshape(E0 * F0C, 128).T, "b1_1": arr("L1_ffn_b1").reshape(-1, 128).T,
             "ws1": arr("L1_ffn_Ws1")}
    for l in range(LAYERS):
        parts[f"wq{l}"], parts[f"wk{l}"], parts[f"wv{l}"] = pairs_last(wq[l]), pairs_last(wk[l]), wv[l]
    arrays = {
        "x": x0.reshape(B * S, D),
        "ctxT": arr("ctx_1024").transpose(0, 2, 1),
        "mask": arr("mask_BxSxS2_ik1").reshape(G, T, S2),
        "wpack": np.concatenate([parts[n] for n in COLS], axis=1),
        "bqrow": np.concatenate([pairs_last(arr("L0_xattn_bq")), pairs_last(arr("L1_xattn_wq_bias"))])[None],
        "bcast": np.concatenate([arr("L0_xattn_bo"), arr("L1_xattn_wo_bias"), arr("g_xattn"), arr("g_ffn"),
                                 arr("L1_ffn_route_scale").reshape(1)]),
        "wo": np.stack([arr("L0_xattn_Wo").T, arr("L1_xattn_wo_kernel")]),
        "bvc": np.stack([arr("L0_xattn_bv"), arr("L1_xattn_wv_bias")]).reshape(LAYERS, 2, 4, PR).transpose(0, 2, 3, 1),
        "w1_0": arr("L0_ffn_w1"), "w2_0": arr("L0_ffn_w2"), "b2_0": arr("L0_ffn_b2"),
        "w1_1": arr("L1_ffn_W1"), "w2_1": arr("L1_ffn_W2"),
        "b2_1": np.concatenate([arr("L1_ffn_b2"), arr("L1_ffn_bs2")[None]]),
        "ws2": arr("L1_ffn_Ws2"), "bs1": arr("L1_ffn_bs1")[:, None],
    }
    nc = bacc.Bacc("TRN2", target_bir_lowering=False, num_devices=1)
    given, args = {}, []
    for name, a in arrays.items():
        a = np.ascontiguousarray(a)
        given[f"in_{name}"] = a
        args.append(nc.dram_tensor(f"in_{name}", a.shape, mybir.dt.from_np(a.dtype), kind="ExternalInput").ap())
    args.append(nc.dram_tensor("out_0", (B * S, D), F32, kind="ExternalOutput").ap())
    build(nc, *args)
    r = run_bass_kernel_spmd(nc, [given], core_ids=[0])
    return r.results[0]["out_0"].reshape(B, S, D)
```

```python
from contextlib import ExitStack

import concourse.bass as bass
from concourse import mybir

ALU = mybir.AluOpType
ACT = mybir.ActivationFunctionType
AX = mybir.AxisListType
F32 = mybir.dt.float32
F16 = mybir.dt.float16
I32 = mybir.dt.int32

LAYERS = 2
B, S, D, S2 = 16, 56, 128, 1500
H = 16
HD = D // H
PAIRS = H // 2
PR = 2 * HD
G = B // 2
T = 2 * S
NB = LAYERS * B
KT, KP = 12, 125
CH, CW = 3, 500
KPC = CW // KP
MASK0 = 3 * PR
SHIFT0 = MASK0 + S
ROWS = SHIFT0 + 2
RING = 3
NMAX = CH * PAIRS
MAXES_PER_KT = NMAX // KT
E_LAG = 3
AV_LAG = E_LAG + 2
QK_SCALE = 4.0
EXP_SCALE = 1.0 / (QK_SCALE * QK_SCALE * float(HD) ** 0.5)
BIG = 32768.0
EPS = 1e-5
E0, F0C = 8, 4
E1, F1 = 8, 64
NE = 8

COLS = {}
_at = 0
for _name, _n in (("wq0", D), ("wq1", D), ("wk0", D), ("wv0", D), ("wk1", D), ("wv1", D),
                  ("bk0", 1), ("bk1", 1), ("gate0", NE), ("gate1", NE), ("b1_0", E0 * F0C),
                  ("b1_1", E1 * F1 // 128), ("ws1", F1)):
    COLS[_name] = (_at, _at + _n)
    _at += _n
NCOLS = _at
BO, GX, GF, RS, NBC = 0, 2 * D, 2 * D + 2, 2 * D + 4, 2 * D + 5


def has_k(s):
    return -1 <= s <= NB - 2


def has_v(s):
    return 0 <= s <= NB - 1


def has_m(s):
    return 0 <= s <= NB - 1


def has_q(s):
    return s % 2 == 1 and -1 <= s <= NB - 3


def has_a(s):
    return s % 2 == 1 and 3 <= s <= NB + 1


def has_f(s):
    return s % 2 == 0 and 4 <= s <= NB + 2


def has_end(s):
    return s % 2 == 1 and 5 <= s <= NB + 3


def has_mask(s):
    return s == 4 or s % 2 == 0 and B <= s <= NB - 4


def is_batch(n):
    return 0 <= n < NB


def layer_of(n):
    return n // B


def tile_at(kt, lag):
    return (1, kt - lag) if kt >= lag else (2, kt - lag + KT)


def kv_uses(s):
    uses = []
    if has_k(s):
        uses += [(2, "k0", 1), (4, "k1", 1), (6, "k2", 1)]
    if has_v(s):
        uses += [(8, "v0", 1), (9, "v1", 1), (10, "v2", 1)]
    return uses


def fh_uses(s):
    uses = []
    if has_q(s):
        uses += [(4, "qT", 2), (5 if s < 0 else 6, "q", 1)]
    if has_a(s):
        uses += [(10, "h0", 1), (11, "h1", 1)]
    if has_f(s) and layer_of(s - 3) == 0:
        uses += [(e - 2, f"h{e}", 1) for e in range(2, 8)]
    return uses


def fy_uses(s):
    uses = []
    if has_m(s - 1):
        uses.append((0, "ct", 1))
    if has_end(s):
        uses += [(1, "y3", 1), (3, "yb", 1)]
    if is_batch(s - 2):
        uses.append((5, "sum", 1))
    if has_a(s):
        uses += [(7, "y", 1), (9, "xT", 1), (10, "lg", 1)]
    if has_f(s):
        uses += [(7, "gT", 1)] + [(9 + i, f"y{i}", 1) for i in range(3)]
    return sorted(uses, key=lambda u: u[0])


def issued_before(uses, s, kt):
    if kt > 0:
        return [(0, u[1]) for u in uses(s) if u[0] == kt - 1]
    return [(1, u[1]) for u in uses(s - 1) if u[0] == KT - 1]


def experts_of(i):
    e = 4 * (i // 2) + i % 2
    return e, e + 2


def before(uses, s, freed=False):
    return sum(u[2] if freed else 1 for t in range(-1, s) for u in uses(t))


def upto(uses, s, name, freed=False):
    n = before(uses, s, freed)
    for u in uses(s):
        n += u[2] if freed else 1
        if u[1] == name:
            return n
    raise KeyError((s, name))


def links(s):
    n = 0
    if has_m(s - 1):
        n += 2
    if has_q(s):
        n += 2
    if has_a(s):
        n += 2 + (layer_of(s - 2) == 0)
    if has_f(s):
        n += 9 + (layer_of(s - 3) == 1) + 2
    if has_end(s):
        n += 2
    return n


def b_total(n):
    return 48 * min(n + 1, B) + 64 * max(0, n + 1 - B)


class Step:

    def __init__(self, s0, turn=None, turns=1):
        self.s, self.turn, self.turns = s0, turn, turns

    def at(self, f):
        v = f(self.s)
        if self.turn is None:
            return v
        d = f(self.s + 2) - v
        assert all(f(self.s + 2 * i) == v + i * d for i in range(self.turns))
        return v + self.turn * d if d else v


PEELED_AND_LOOPS = [-1, 0, 1, 2, 3, 4, (5, 5), 15, 16, 17, 18, 19, 20, (21, 4), 29, 30, 31, 32, 33, 34, 35]


def run_steps(eng, step):
    for item in PEELED_AND_LOOPS:
        if isinstance(item, tuple):
            s0, turns = item
            with eng.Fori(0, turns) as turn:
                step(Step(s0, turn, turns))
                step(Step(s0 + 1, turn, turns))
        else:
            step(Step(item))


def build(nc, x, ctxT, mask, wpack, bqrow, bcast, wo, bvc, w1_0, w2_0, b2_0, w1_1, w2_1, b2_1, ws2, bs1, out):
    with ExitStack() as ctx:
        def sb(name, shape, dt=F32):
            return ctx.enter_context(nc.sbuf_tensor(name, shape, dt))

        def ps(name, shape):
            return ctx.enter_context(nc.psum_tensor(name, shape, F32))

        def sem(name):
            return ctx.enter_context(nc.semaphore(name))

        W = sb("W", [128, NCOLS])

        def w(name):
            a, b = COLS[name]
            return W[:, a:b]

        bq_row = sb("bq_row", [1, LAYERS * D])
        bc = sb("bc", [128, NBC])
        gains = sb("gains", [128, 4])
        tbo = sb("tbo", [T, LAYERS, D])
        woE = sb("woE", [128, LAYERS, 2, D])
        bvE = sb("bvE", [128, LAYERS, 2])
        w1a = sb("w1a", [128, E0, F0C * 128])
        w2a = sb("w2a", [128, E0, F0C, D])
        w1b = sb("w1b", [128, E1, F1])
        w2b = sb("w2b", [128, E1 // 2, D])
        ws2b = sb("ws2b", [F1, D])
        bs1b = sb("bs1b", [F1, 1])
        b2x = sb("b2x", [NE + 1, LAYERS, D])
        ident = sb("ident", [128, 128])
        ident16 = sb("ident16", [128, 128], F16)
        sel = sb("sel", [128, 128])
        rowmask = sb("rowmask", [128, 4])
        headmask = sb("headmask", [128, 2, 2, S])
        bvm = sb("bvm", [128, LAYERS, 2, 2, S])
        ones = sb("ones", [128, T])
        before_me = sb("before_me", [T, NE, NE])
        mhalf = sb("mhalf", [T, 1])

        X = sb("X", [T, G * D])
        C = sb("C", [128, S2])
        Chi = sb("Chi", [128, 2, S2], F16)
        Clo = sb("Clo", [128, 2, S2], F16)
        Whi = sb("Whi", [128, LAYERS, 2, D], F16)
        Wlo = sb("Wlo", [128, LAYERS, 2, D], F16)
        khi = sb("khi", [128, S2], F16)
        klo = sb("klo", [128, S2], F16)
        a = COLS["wk0"][0]
        kfull = W[:, a:a + CW]
        kop = sb("kop", [128, 2, PAIRS, S2], F16)
        qmax = sb("qmax", [128, 2, PAIRS, 2, S], F16)
        qexp = sb("qexp", [128, 2, PAIRS, 2, S], F16)
        V = sb("V", [128, 2, KT, PAIRS, 32])
        P = sb("P", [128, RING, PAIRS * T])
        pick = P[0:S, 0, 0:H * S // 2].bitcast(F16).rearrange("s (h q) -> s h q", h=H)
        maskin = sb("maskin", [T, S2], I32)
        maskop = sb("maskop", [T, S2], F16)
        shift_rows = maskin[0:1, :].bitcast(F16).rearrange("a (i n) -> a i n", i=2)
        maskraw = sb("maskraw", [T, S2], F16)
        masksink = maskin[:, 0:S2 // 2].bitcast(F16)
        masksum = sb("masksum", [T, 1])
        keep = sb("keep", [T, 1])
        stq, mvq = sb("stq", [T, 6]), sb("mvq", [T, 2])
        stf, mvf = sb("stf", [T, 6]), sb("mvf", [T, 2])
        veq, rsq, rkq = sb("veq", [T, 1]), sb("rsq", [T, 1]), sb("rkq", [T, 1])
        vef, rsf = sb("vef", [T, 1]), sb("rsf", [T, 1])
        xnq = sb("xnq", [T, D])
        xnqT = sb("xnqT", [128, T])
        keepT = sb("keepT", [1, T])
        qhi = sb("qhi", [128, T], F16)
        qlo = sb("qlo", [128, T], F16)
        mx = sb("mx", [T, 2, CH, PAIRS])
        m8 = sb("m8", [T, PAIRS])
        cc = sb("cc", [T, 2, PAIRS], F16)
        ct = sb("ct", [2 * PAIRS, T], F16)
        OM = sb("OM", [128, 2, 2 * T])
        rden = sb("rden", [128, 2 * T])
        ON0 = sb("ON0", [128, 2 * T])
        ON = sb("ON", [128, 2, 2, 2, S])
        XF0, XF = sb("XF0", [T, D]), sb("XF", [T, D])
        xnf = sb("xnf", [T, D])
        xnfT = sb("xnfT", [128, T])
        lg = sb("lg", [T, NE])
        lmax, lneg = sb("lmax", [T, 1]), sb("lneg", [T, 1])
        ge, gse = sb("ge", [T, NE]), sb("gse", [T, 1])
        g1, g2 = sb("g1", [T, NE]), sb("g2", [T, NE])
        gp = sb("gp", [T, NE])
        ggt, geq, gel, grk = (sb(n, [T, NE, NE]) for n in ("ggt", "geq", "gel", "grk"))
        rank, gsp = sb("rank", [T, NE]), sb("gsp", [T, NE])
        gden, grd = sb("gden", [T, 1]), sb("grd", [T, 1])
        gate = sb("gate", [T, NE + 1])
        gateT = sb("gateT", [NE + 1, T])
        HR = sb("HR", [128, E0 * F0C, T])
        acc = sb("acc", [T, 2, D])

        pMX = ps("pMX", [128, 2, 512])
        pST = ps("pST", [128, 2, 512])
        pO = ps("pO", [128, 512])
        pKV = ps("pKV", [128, 512])
        pFH = ps("pFH", [128, 512])
        pFY = ps("pFY", [128, 512])

        w_in, x_in, f_in, f2_in, f3_in, wo_in = sem("w_in"), sem("x_in"), sem("f_in"), sem("f2_in"), sem("f3_in"), sem("wo_in")
        c_in = sem("c_in")
        init_c = sem("init_c")
        init_chi = sem("init_chi")
        chi_done = sem("chi_done")
        ctx_split = sem("ctx_split")
        mask_in = sem("mask_in")
        init_p = sem("init_p")
        init_v = sem("init_v")
        init_l = sem("init_l")
        init_w = sem("init_w")
        init_a = sem("init_a")
        init_dma = sem("init_dma")
        kop_in = [sem(f"kop_in{c}") for c in range(CH)]
        qmax_in = sem("qmax_in")
        qexp_in = [sem("qexp_in0"), sem("qexp_in1")]
        shift_in = sem("shift_in")
        mask_done, masksum_done, keep_done = sem("mask_done"), sem("masksum_done"), sem("keep_done")
        maskop_done = sem("maskop_done")
        khi_done, klo_done = sem("khi_done"), sem("klo_done")
        kv_ready, kv_free = sem("kv_ready"), sem("kv_free")
        mx_ready, max_done = sem("mx_ready"), sem("max_done")
        cc_ready = sem("cc_ready")
        st_ready, exp_done = sem("st_ready"), sem("exp_done")
        av_done, o_free = sem("av_done"), sem("o_free")
        fh_ready, fh_free = sem("fh_ready"), sem("fh_free")
        fy_ready, fy_free = sem("fy_ready"), sem("fy_free")
        statq_done, rstdq_done, xnq_done = sem("statq_done"), sem("rstdq_done"), sem("xnq_done")
        statf_done, rstdf_done, xnf_done = sem("statf_done"), sem("rstdf_done"), sem("xnf_done")
        on_done = sem("on_done")
        logit_done, gexp_done, gate_done = sem("logit_done"), sem("gexp_done"), sem("gate_done")
        gelu_done = sem("gelu_done")
        x_done = sem("x_done")
        dve_link, pool_link = sem("dve_link"), sem("pool_link")
        stored = sem("stored")
        passed = sem("passed")

        block = ctx.enter_context(nc.Block())

        def apart(eng):
            eng.sem_inc(passed, 1)

        def groups(f):
            return lambda s: sum(f(t) for t in range(-1, s))

        q_count, a_count, f_count = groups(has_q), groups(has_a), groups(has_f)

        mask_count = groups(lambda t: has_q(t) and t + 1 >= B)
        maskraw_count = groups(has_mask)

        @block.sync
        def _(sp):
            sp.dma_start(W[:, :], wpack).then_inc(w_in, 16)
            sp.dma_start(bq_row[:, :], bqrow).then_inc(w_in, 16)
            sp.dma_start(bc[:, :], bcast.partition_broadcast(128)).then_inc(w_in, 16)
            sp.dma_start(C[:, :], ctxT[0]).then_inc(c_in, 16)
            sp.dma_start(X[:, :].rearrange("t (g d) -> t g d", g=G),
                         x.rearrange("(g t) d -> t g d", g=G)).then_inc(x_in, 16)
            sp.wait_ge(init_v, 1)
            sp.wait_ge(init_p, 5)
            for b in range(2):
                sp.dma_start(kop[MASK0:SHIFT0, b, :, :],
                             maskop[0:S, :].unsqueeze(1).broadcast_to([S, PAIRS, S2])).then_inc(init_dma, 16)
                for i in range(2):
                    sp.dma_start(kop[SHIFT0 + i:SHIFT0 + i + 1, b, :, :],
                                 shift_rows[:, i:i + 1, :].broadcast_to([1, PAIRS, S2])).then_inc(init_dma, 16)
                sp.dma_start(qmax[MASK0:SHIFT0, b, :, :, :],
                             pick[:, :, :].rearrange("s (p j) q -> s p j q", j=2)).then_inc(init_dma, 16)

            def late_loads(s):
                if s == 0:
                    sp.wait_ge(init_w, 3)
                    for g in range(4):
                        rows = slice(32 * g, 32 * g + PR)
                        sp.dma_start(woE[rows, :, :, :], wo.rearrange("l (r g i) n -> g i l r n", r=2, g=4)[g]
                                     ).then_inc(wo_in, 16)
                        sp.dma_start(bvE[rows, :, :], bvc.rearrange("l g i r -> g i l r")[g]).then_inc(wo_in, 16)
                if s == 1:
                    sp.dma_start(b2x[0:NE, 0, :], b2_0).then_inc(f_in, 16)
                    sp.dma_start(b2x[:, 1, :], b2_1).then_inc(f_in, 16)
                    sp.dma_start(ws2b[:, :], ws2).then_inc(f_in, 16)
                    sp.dma_start(bs1b[:, :], bs1).then_inc(f_in, 16)
                    sp.dma_start(w1a[:, 0:E0 // 2, :], w1_0[0:E0 // 2].rearrange("e d f -> d e f")).then_inc(f_in, 16)
                    sp.wait_ge(init_dma, 128)
                    sp.dma_start(maskin[:, :], mask[0]).then_inc(mask_in, 16)
                if s == 2:
                    sp.dma_start(w1a[:, E0 // 2:, :], w1_0[E0 // 2:].rearrange("e d f -> d e f")).then_inc(f2_in, 16)
                    sp.dma_start(w1b[:, :, :], w1_1.rearrange("e d f -> d e f")).then_inc(f2_in, 16)
                    sp.dma_start(w2b[:, :, :], w2_1.rearrange("(c e) f d -> (e f) c d", e=2)).then_inc(f2_in, 16)
                if s == 3:
                    for half in (slice(0, E0 // 2), slice(E0 // 2, E0)):
                        sp.dma_start(w2a[:, half, :, :], w2_0[half].rearrange("e (c f) d -> f e c d", c=F0C)
                                     ).then_inc(f3_in, 16)

            def key_chunk(st, ahead, c):
                n, cols = st.s + ahead, slice(c * CW, (c + 1) * CW)
                dst = n % 2
                sp.wait_ge(klo_done, st.at(lambda s: CH * (s + ahead) + c + 1))
                apart(sp)
                if n >= 2:
                    sp.wait_ge(st_ready, st.at(lambda s: 2 * (KT * (s + ahead - 2) + KPC * (c + 1))))
                    apart(sp)
                if n >= B and n % 2 == 0:
                    sp.wait_ge(maskop_done, st.at(lambda s: CH * ((s + ahead - B) // 2) + c + 1))
                    apart(sp)
                for row, part in ((0, khi), (PR, klo), (2 * PR, khi)):
                    sp.dma_start(kop[row:row + PR, dst, :, cols], part[:, cols]).then_inc(kop_in[c], 16)
                if n >= B:
                    half = S * (n % 2)
                    sp.dma_start(kop[MASK0:SHIFT0, dst, :, cols],
                                 maskop[half:half + S, cols].unsqueeze(1).broadcast_to([S, PAIRS, CW])
                                 ).then_inc(kop_in[c], 16)

            def step(st):
                s = st.s
                if has_m(s - 1):
                    sp.wait_ge(fy_free, st.at(lambda s: upto(fy_uses, s, "ct", True)))
                    apart(sp)
                    sp.dma_start(qexp[SHIFT0:ROWS, (s - 1) % 2, :, :, :].rearrange("r p j q -> r (p j q)"),
                                 ct[:, :]).then_inc(shift_in, 16)
                if has_k(s - 1):
                    key_chunk(st, 0, 2)
                if has_m(s):
                    if s == 0:
                        sp.wait_ge(init_dma, 128)
                    sp.wait_ge(qmax_in, st.at(lambda s: 96 * (s + 1)))
                    apart(sp)
                    if is_batch(s - 2):
                        sp.wait_ge(st_ready, st.at(lambda s: 2 * KT * (s - 1)))
                        apart(sp)
                    sp.dma_start(qexp[0:SHIFT0, s % 2, :, :, :], qmax[0:SHIFT0, s % 2, :, :, :]).then_inc(qexp_in[s % 2], 16)
                if s <= NB - 3:
                    if s == -1:
                        sp.wait_ge(init_c, 2 * LAYERS + CH)
                    else:
                        sp.wait_ge(ctx_split, st.at(lambda s: CH * (s + 1)))
                    apart(sp)
                    if st.turn is None:
                        src = ctxT[(s + 2) % B]
                    else:
                        src = ctxT[bass.ds(st.at(lambda s: s + 2 - (B if st.s >= B else 0)) & (B - 1), 1)].rearrange("a d k -> (a d) k")
                    sp.dma_start(C[:, :], src).then_inc(c_in, 16)
                if has_k(s):
                    key_chunk(st, 1, 0)
                    if has_q(s):
                        sp.wait_ge(fh_free, st.at(lambda s: upto(fh_uses, s, "q", True)))
                        apart(sp)
                    if s >= 1:
                        sp.wait_ge(mx_ready, st.at(lambda s: NMAX * s))
                        apart(sp)
                        sp.wait_ge(qexp_in[(s - 1) % 2], st.at(lambda s: 16 * ((s - 1) // 2 + 1)))
                        apart(sp)
                    half = S * ((s + 1) % 2)
                    for row, part in ((0, qhi), (PR, qhi), (2 * PR, qlo)):
                        for j in range(2):
                            sp.dma_start(qmax[row + HD * j:row + HD * (j + 1), (s + 1) % 2, :, j, :],
                                         part[64 * j:64 * (j + 1), half:half + S]).then_inc(qmax_in, 16)
                if s >= B - 1 and has_mask(s + 1):
                    group = st.at(lambda s: (s + 3 - B) // 2)
                    sp.wait_ge(masksum_done, st.at(lambda s: mask_count(s) + 1))
                    apart(sp)
                    src = mask[group] if isinstance(group, int) else mask[bass.ds(group, 1)].rearrange("a t k -> (a t) k")
                    sp.dma_start(maskin[:, :], src).then_inc(mask_in, 16)
                if has_k(s):
                    key_chunk(st, 1, 1)
                late_loads(s)

            run_steps(sp, step)
            sp.wait_ge(x_done, 2 * G - 1)
            sp.dma_start(out[0:(G - 1) * T, :].rearrange("(g t) d -> t g d", g=G - 1),
                         X[:, 0:(G - 1) * D].rearrange("t (g d) -> t g d", g=G - 1)).then_inc(stored, 16)
            sp.wait_ge(x_done, 2 * G)
            sp.dma_start(out[(G - 1) * T:, :], X[:, (G - 1) * D:]).then_inc(stored, 16)
            sp.wait_ge(stored, 32)

        @block.gpsimd
        def _(pool):
            nc.gpsimd.memset(shift_rows[:, 0, :], -BIG).then_inc(init_p, 1)
            nc.gpsimd.memset(shift_rows[:, 1, :], -1.0).then_inc(init_p, 1)
            nc.gpsimd.memset(maskop[:, :], 0.0).then_inc(init_p, 1)
            nc.gpsimd.memset(pick[:, :, :], 0.0).then_inc(init_p, 1)
            pool.wait_ge(init_p, 4)
            nc.gpsimd.affine_select(out=pick[:, :, :], in_=pick[:, :, :], compare_op=ALU.not_equal, fill=BIG,
                                    base=0, pattern=[[0, H], [-1, S]], channel_multiplier=1).then_inc(init_p, 1)
            nc.gpsimd.memset(ident[:, :], 0.0).then_inc(init_p, 1)
            nc.gpsimd.memset(ident16[:, :], 0.0).then_inc(init_p, 1)
            nc.gpsimd.memset(sel[:, :], 0.0).then_inc(init_p, 1)
            nc.gpsimd.memset(before_me[:, :, :], 1.0).then_inc(init_p, 1)
            nc.gpsimd.memset(mhalf[:, :], -0.5).then_inc(init_p, 1)
            nc.gpsimd.memset(keep[:, :], 1.0).then_inc(init_p, 1)
            pool.wait_ge(init_p, 11)
            for m in (ident, ident16):
                nc.gpsimd.affine_select(out=m[:, :], in_=m[:, :], compare_op=ALU.not_equal, fill=1.0,
                                        base=0, pattern=[[-1, 128]], channel_multiplier=1).then_inc(init_p, 1)
            nc.gpsimd.affine_select(out=sel[:, :].rearrange("p (g i) -> p g i", g=4),
                                    in_=sel[:, :].rearrange("p (g i) -> p g i", g=4),
                                    compare_op=ALU.not_equal, fill=1.0, base=-PR,
                                    pattern=[[-32, 4], [0, 32]], channel_multiplier=1).then_inc(init_p, 1)
            nc.gpsimd.affine_select(out=before_me[:, :, :], in_=before_me[:, :, :], compare_op=ALU.is_gt, fill=0.0,
                                    base=0, pattern=[[1, NE], [-1, NE]], channel_multiplier=0).then_inc(init_p, 1)
            linked = [0]

            def link(ins):
                linked[0] += 1
                ins.then_inc(pool_link, 1)

            def pool_links(s):
                return sum(2 * has_q(t) + is_batch(t - 2) + has_a(t) for t in range(-1, s))

            def low_part(st, c):
                if not has_k(st.s):
                    return
                cols = slice(c * CW, (c + 1) * CW)
                pool.wait_ge(khi_done, st.at(lambda s: CH * (s + 1) + c + 1))
                apart(pool)
                pool.wait_ge(kv_free, st.at(lambda s: upto(kv_uses, s, f"k{c}", True)))
                apart(pool)
                nc.gpsimd.tensor_tensor(klo[:, cols], kfull, khi[:, cols], ALU.subtract).then_inc(klo_done, 1)

            def mask_part(st, c):
                if has_q(st.s) and st.s + 1 >= B:
                    cols = slice(c * CW, (c + 1) * CW)
                    pool.wait_ge(kop_in[c], st.at(b_total))
                    apart(pool)
                    nc.gpsimd.tensor_copy(maskop[:, cols], maskraw[:, cols]).then_inc(maskop_done, 1)

            def step(st):
                s = st.s
                if has_q(s):
                    pool.wait_ge(statq_done, st.at(lambda s: q_count(s) + 1))
                    apart(pool)
                    nc.gpsimd.tensor_scalar(veq[:, :], mvq[:, 1:2], EPS, None, ALU.add).then_inc(pool_link, 1)
                    pool.wait_ge(pool_link, st.at(lambda s: pool_links(s) + 1))
                    nc.gpsimd.tensor_tensor(rsq[:, :], veq[:, :], mhalf[:, :], ALU.pow).then_inc(pool_link, 1)
                    pool.wait_ge(pool_link, st.at(lambda s: pool_links(s) + 2))
                    if s + 1 >= B:
                        pool.wait_ge(keep_done, st.at(lambda s: mask_count(s) + 1))
                    nc.gpsimd.tensor_tensor(rkq[:, :], rsq[:, :], keep[:, :], ALU.mult).then_inc(rstdq_done, 1)
                low_part(st, 0)
                mask_part(st, 0)
                low_part(st, 1)
                mask_part(st, 1)
                if is_batch(s - 2):
                    l, n = layer_of(s - 2), 2 * has_q(s) + 1
                    pool.wait_ge(fy_free, st.at(lambda s: upto(fy_uses, s, "sum", True)))
                    apart(pool)
                    if s >= 4:
                        pool.wait_ge(fy_ready, st.at(lambda s: upto(fy_uses, s - 2 + (s + 1) % 2, "y")))
                        apart(pool)
                    nc.gpsimd.tensor_tensor(ON0[:, :], OM[:, s % 2, :], rden[:, :], ALU.mult).then_inc(pool_link, 1)
                    pool.wait_ge(pool_link, st.at(lambda s: pool_links(s) + n))
                    nc.gpsimd.tensor_tensor(ON[:, :, :, s % 2, :].rearrange("p r j q -> p (r j) q"),
                                            ON0[:, :].rearrange("p (n q) -> p n q", q=S),
                                            bvm[:, l, :, :, :].rearrange("p r j q -> p (r j) q"),
                                            ALU.add).then_inc(on_done, 1)
                mask_part(st, 2)
                low_part(st, 2)
                if has_mask(s):
                    pool.wait_ge(mask_in, st.at(lambda s: 16 * (maskraw_count(s) + 1)))
                    apart(pool)
                    nc.gpsimd.tensor_scalar(maskraw[:, :], maskin[:, :], 0, -BIG, ALU.is_equal, ALU.mult
                                            ).then_inc(mask_done, 1)
                if has_a(s):
                    n = 2 * has_q(s) + 2
                    pool.wait_ge(statf_done, st.at(lambda s: a_count(s) + 1))
                    apart(pool)
                    nc.gpsimd.tensor_scalar(vef[:, :], mvf[:, 1:2], EPS, None, ALU.add).then_inc(pool_link, 1)
                    pool.wait_ge(pool_link, st.at(lambda s: pool_links(s) + n))
                    nc.gpsimd.tensor_tensor(rsf[:, :], vef[:, :], mhalf[:, :], ALU.pow).then_inc(rstdf_done, 1)
                if s <= NB - 3:
                    for c in range(CH):
                        cols = slice(c * CW, (c + 1) * CW)
                        pool.wait_ge(chi_done, st.at(lambda s: CH * (s + 1) + c + 1))
                        apart(pool)
                        nc.gpsimd.tensor_tensor(Clo[:, s % 2, cols], C[:, cols], Chi[:, s % 2, cols], ALU.subtract
                                                ).then_inc(ctx_split, 1)

            run_steps(pool, step)

        @block.scalar
        def _(act):
            act.wait_ge(c_in, 16)
            for c in range(CH):
                cols = slice(c * CW, (c + 1) * CW)
                nc.scalar.activation(Chi[:, 0, cols], C[:, cols], ACT.Copy).then_inc(init_chi, 1)
            act.wait_ge(w_in, 48)
            nc.scalar.activation(gains[:, :], bc[:, GX:GX + 4], ACT.Tanh).then_inc(init_a, 1)
            act.wait_ge(init_v, 6)

            def exps(st, kt, h):
                back, tile = tile_at(kt, E_LAG)
                if not is_batch(st.s - back):
                    return
                slot = tile % RING
                act.wait_ge(st_ready, st.at(lambda s: 2 * (KT * (s - back) + tile) + h + 1))
                if h == 0 and (st.s > back or tile >= RING):
                    act.wait_ge(av_done, st.at(lambda s: KT * (s - back) + tile - RING + 1))
                nc.scalar.activation(P[0:KP, slot, h * 4 * T:(h + 1) * 4 * T], pST[0:KP, h, 0:4 * T], ACT.Exp,
                                     scale=EXP_SCALE).then_inc(exp_done, 1)

            def step(st):
                s = st.s
                for kt in range(KT):
                    exps(st, kt, 0)
                    for use in [u[1] for u in kv_uses(s) if u[0] == kt]:
                        c = int(use[1])
                        act.wait_ge(kv_ready, st.at(lambda s: upto(kv_uses, s, use)))
                        if use[0] == "k":
                            if s >= 0:
                                act.wait_ge(kop_in[c], st.at(b_total))
                            nc.scalar.activation(khi[:, c * CW:(c + 1) * CW], pKV[:, 0:CW], ACT.Identity,
                                                 bias=w(f"bk{layer_of(s + 1)}"), scale=1.0).then_inc(khi_done, 1)
                        else:
                            if s == 0 and c == 0:
                                act.wait_ge(init_v, 8)
                            if s >= 2:
                                act.wait_ge(av_done, st.at(lambda s: KT * (s - 1)))
                            nc.scalar.activation(
                                V[0:KP, s % 2, 4 * c:4 * c + 4, :, 0:PR].rearrange("k t p i -> k (t p) i"),
                                pKV[0:KP, :].rearrange("k (m i) -> k m i", i=PR), ACT.Copy).then_inc(kv_free, 1)
                    exps(st, kt, 1)
                    for use in [u[1] for u in kv_uses(s) if u[0] == kt and u[1][0] == "k"]:
                        c = int(use[1])
                        if s >= 0 or c > 0:
                            act.wait_ge(klo_done, st.at(lambda s: CH * (s + 1) + c))
                        nc.scalar.activation(kfull, pKV[:, 0:CW], ACT.Identity,
                                             bias=w(f"bk{layer_of(s + 1)}"), scale=1.0).then_inc(kv_free, 1)
                    if kt == 0 and has_q(s) and s + 1 >= B:
                        act.wait_ge(mask_done, st.at(lambda s: mask_count(s) + 1))
                        nc.scalar.activation(masksink, maskraw[:, :], ACT.Copy, accum_out=masksum[:, :]
                                             ).then_inc(masksum_done, 1)
                    if kt == 11 and has_a(s):
                        act.wait_ge(logit_done, st.at(lambda s: a_count(s) + 1))
                        if layer_of(s - 2) == 0:
                            nc.scalar.activation(ge[:, :], lg[:, :], ACT.Exp, bias=lneg[:, :], scale=1.0,
                                                 accum_out=gse[:, :]).then_inc(gexp_done, 1)
                        else:
                            nc.scalar.activation(ge[:, :], lg[:, :], ACT.Exp, scale=-1.0).then_inc(gexp_done, 1)
                    if kt >= KT - CH and s <= NB - 3:
                        c = kt - (KT - CH)
                        if c == 0:
                            act.wait_ge(c_in, st.at(lambda s: 16 * (s + 3)))
                        if s >= 0:
                            act.wait_ge(kv_ready, st.at(lambda s: upto(kv_uses, s, f"v{c}")))
                        nc.scalar.activation(Chi[:, s % 2, c * CW:(c + 1) * CW], C[:, c * CW:(c + 1) * CW], ACT.Copy
                                             ).then_inc(chi_done, 1)
                    if kt == 8 and has_f(s):
                        act.wait_ge(fh_free, st.at(lambda s: before(fh_uses, s + 1, True)))
                        if layer_of(s - 3) == 0:
                            nc.scalar.activation(HR[:, :, :], HR[:, :, :], ACT.Gelu).then_inc(gelu_done, 2)
                        else:
                            nc.scalar.activation(HR[:, 0:4, :], HR[:, 0:4, :], ACT.Gelu).then_inc(gelu_done, 1)
                            nc.scalar.activation(HR[0:F1, 4, :], HR[0:F1, 4, :], ACT.Gelu).then_inc(gelu_done, 1)

            run_steps(act, step)

        @block.vector
        def _(dve):
            nc.vector.memset(qmax[:, :, :, :, :].rearrange("p b r j q -> p (b r j q)"), 0.0).then_inc(init_v, 1)
            Vf = V[:, :, :, :, :].rearrange("k b t p i -> k (b t p) i")
            nc.vector.memset(Vf[:, :, PR:PR + 1], 1.0).then_inc(init_v, 1)
            nc.vector.memset(woE[:, :, :, :], 0.0).then_inc(init_w, 1)
            nc.vector.memset(bvE[:, :, :], 0.0).then_inc(init_w, 1)
            nc.vector.memset(b2x[:, 0, :], 0.0).then_inc(init_w, 1)
            dve.wait_ge(w_in, 48)
            for name, width in (("wq0", 2 * D), ("wk0", D), ("wk1", D), ("bk0", 2)):
                a = COLS[name][0]
                nc.vector.tensor_scalar(W[:, a:a + width], W[:, a:a + width], QK_SCALE, None, ALU.mult).then_inc(init_v, 1)
            nc.vector.tensor_scalar(bq_row[:, :], bq_row[:, :], QK_SCALE, None, ALU.mult).then_inc(init_v, 1)
            dve.wait_ge(init_v, 5)
            for l in range(LAYERS):
                a = COLS[f"wk{l}"][0]
                kv = W[:, a:a + 2 * D]
                nc.vector.tensor_copy(Whi[:, l, :, :].rearrange("p m n -> p (m n)"), kv).then_inc(init_c, 1)
                dve.wait_ge(init_c, 2 * l + 1)
                nc.vector.tensor_tensor(Wlo[:, l, :, :].rearrange("p m n -> p (m n)"), kv,
                                        Whi[:, l, :, :].rearrange("p m n -> p (m n)"), ALU.subtract).then_inc(init_c, 1)
            for c in range(CH):
                cols = slice(c * CW, (c + 1) * CW)
                dve.wait_ge(init_chi, c + 1)
                nc.vector.tensor_tensor(Clo[:, 0, cols], C[:, cols], Chi[:, 0, cols], ALU.subtract).then_inc(init_c, 1)
            dve.wait_ge(init_p, 15)
            dve.wait_ge(x_in, 16)

            def late_constants():
                nc.vector.memset(ones[:, :], 1.0).then_inc(init_l, 1)
                nc.vector.memset(gate[:, NE:NE + 1], 1.0).then_inc(init_l, 1)
                ig = ident[:, :].rearrange("p (g i) -> p g i", g=4)
                for k, (a, b) in enumerate(((0, HD), (HD, PR), (PR, PR + 1))):
                    nc.vector.tensor_reduce(rowmask[:, k:k + 1], ig[:, :, a:b], AX.XY, ALU.add).then_inc(init_l, 1)
                dve.wait_ge(init_l, 5)
                dve.wait_ge(wo_in, 16 * 8)
                dve.wait_ge(init_a, 1)
                for j in range(2):
                    for l in range(LAYERS):
                        for r in range(2):
                            nc.vector.tensor_scalar(bvm[:, l, r, j, :], ones[:, 0:S], rowmask[:, j:j + 1],
                                                    bvE[:, l, r:r + 1], ALU.mult, ALU.mult).then_inc(init_l, 1)
                    nc.vector.tensor_scalar(headmask[:, :, j, :], ones[:, :].rearrange("p (r q) -> p r q", r=2),
                                            rowmask[:, j:j + 1], rowmask[:, 2:3], ALU.mult, ALU.add).then_inc(init_l, 1)
                for l in range(LAYERS):
                    nc.vector.tensor_scalar(tbo[:, l, :], bc[0:T, BO + l * D:BO + (l + 1) * D], gains[0:T, l:l + 1], None,
                                            ALU.mult).then_inc(init_l, 1)
                dve.wait_ge(init_l, 17)

            def links_before(s):
                return sum(links(t) for t in range(-1, s))

            def step(st):
                s = st.s
                linked = [0]

                def link(ins, alone=False):
                    linked[0] += 1
                    k = linked[0]
                    ins.then_inc(dve_link, 1)
                    dve.wait_ge(dve_link, st.at(lambda s: links_before(s) + k))
                    if alone:
                        apart(dve)

                def xg(f):
                    v = st.at(lambda s: D * (f(s) % G))
                    return X[:, bass.ds(v, D)] if st.turn is not None else X[:, v:v + D]

                def ready(sem_, uses, back, name):
                    dve.wait_ge(sem_, st.at(lambda s: upto(uses, s - back, name)))

                def freed(sem_, uses, back, name):
                    dve.wait_ge(sem_, st.at(lambda s: upto(uses, s - back, name, True)))

                def hidden(back, use):
                    e, t = int(use[1]), s - back
                    ready(fh_ready, fh_uses, back, use)
                    if layer_of(t - 2 if has_a(t) else t - 3) == 0:
                        nc.vector.tensor_tensor(
                            HR[:, F0C * e:F0C * (e + 1), :], pFH[:, 0:F0C * T].rearrange("p (c t) -> p c t", c=F0C),
                            w("b1_0")[:, F0C * e:F0C * (e + 1)].unsqueeze(2).broadcast_to([128, F0C, T]),
                            ALU.add).then_inc(fh_free, 1)
                    elif e == 0:
                        nc.vector.tensor_tensor(
                            HR[:, 0:4, :], pFH[:, 0:4 * T].rearrange("p (c t) -> p c t", c=4),
                            w("b1_1").unsqueeze(2).broadcast_to([128, 4, T]), ALU.add).then_inc(fh_free, 1)
                    else:
                        nc.vector.tensor_scalar(HR[0:F1, 4, :], pFH[0:F1, 0:T], bs1b[:, 0:1], None, ALU.add
                                                ).then_inc(fh_free, 1)

                def from_fh(back, use):
                    if use == "qT":
                        ready(fh_ready, fh_uses, back, use)
                        nc.vector.tensor_copy(xnqT[:, :], pFH[:, 0:T]).then_inc(fh_free, 1)
                        nc.vector.tensor_copy(keepT[:, :], pFH[0:1, 128:128 + T]).then_inc(fh_free, 1)
                    elif use == "q":
                        ready(fh_ready, fh_uses, back, use)
                        if s > 0:
                            dve.wait_ge(qmax_in, st.at(lambda s: 96 * (s + 1)))
                        link(nc.vector.tensor_copy(qhi[:, :], pFH[:, 0:T]))
                        nc.vector.tensor_tensor(qlo[:, :], pFH[:, 0:T], qhi[:, :], ALU.subtract).then_inc(fh_free, 1)
                    else:
                        hidden(back, use)

                def from_fy(back, use):
                    ready(fy_ready, fy_uses, back, use)
                    l = layer_of(s - back - 2)
                    if use == "ct":
                        if s > 1:
                            dve.wait_ge(shift_in, st.at(lambda s: 16 * (s - 1)))
                        nc.vector.tensor_copy(ct[:, :], pFY[0:2 * PAIRS, 0:T // 2].bitcast(F16)).then_inc(fy_free, 1)
                    elif use == "sum":
                        if s > 2:
                            dve.wait_ge(on_done, st.at(lambda s: s - 2))
                        nc.vector.reciprocal(rden[:, :], pFY[:, 0:2 * T]).then_inc(fy_free, 1)
                    elif use == "y":
                        nc.vector.scalar_tensor_tensor(out=XF0[:, :], in0=pFY[0:T, 0:D], scalar=gains[0:T, l:l + 1],
                                                       in1=xg(lambda s: (s - 3) // 2), op0=ALU.mult, op1=ALU.add
                                                       ).then_inc(fy_free, 1)
                        freed(fy_free, fy_uses, back, use)
                        link(nc.vector.tensor_tensor(XF[:, :], XF0[:, :], tbo[:, l, :], ALU.add))
                        link(nc.vector.bn_stats(stf[:, :], XF[:, :]), alone=True)
                        nc.vector.bn_aggr(mvf[:, :], stf[:, :]).then_inc(statf_done, 1)
                    elif use == "xT":
                        nc.vector.tensor_copy(xnfT[:, :], pFY[:, 0:T]).then_inc(fy_free, 1)
                    elif use == "lg":
                        nc.vector.tensor_copy(lg[:, :], pFY[0:T, 0:NE]).then_inc(fy_free, 1)
                        freed(fy_free, fy_uses, back, use)
                        if l == 0:
                            link(nc.vector.tensor_reduce(lmax[:, :], lg[:, :], AX.X, ALU.max))
                        nc.vector.tensor_scalar(lneg[:, :], lmax[:, :] if l == 0 else lg[:, 0:1], -1.0, None,
                                                ALU.mult).then_inc(logit_done, 1)
                    elif use == "gT":
                        nc.vector.tensor_copy(gateT[:, :], pFY[0:NE + 1, 0:T]).then_inc(fy_free, 1)
                    elif use == "yb":
                        l = layer_of(s - 4)
                        nc.vector.tensor_tensor(acc[:, 0, :], pFY[0:T, 0:D], acc[:, 1, :], ALU.add).then_inc(fy_free, 1)
                        freed(fy_free, fy_uses, back, use)
                        nc.vector.scalar_tensor_tensor(out=xg(lambda s: (s - 5) // 2), in0=acc[:, 0, :],
                                                       scalar=gains[0:T, 2 + l:3 + l], in1=XF[:, :],
                                                       op0=ALU.mult, op1=ALU.add).then_inc(x_done, 1)
                    else:
                        for j, e in enumerate(experts_of(int(use[1]))):
                            y = pFY[0:T, j * D:(j + 1) * D]
                            if e == 0:
                                ins = nc.vector.tensor_scalar(acc[:, 0, :], y, gate[:, 0:1], None, ALU.mult)
                            else:
                                ins = nc.vector.scalar_tensor_tensor(out=acc[:, j, :], in0=y, scalar=gate[:, e:e + 1],
                                                                     in1=acc[:, 1 - j, :], op0=ALU.mult, op1=ALU.add)
                            if j:
                                ins.then_inc(fy_free, 1)
                                freed(fy_free, fy_uses, back, use)
                            else:
                                link(ins)

                def shares(kt):
                    pj = gp[:, :].unsqueeze(1).broadcast_to([T, NE, NE])
                    pe_ = gp[:, :].unsqueeze(2).broadcast_to([T, NE, NE])
                    if kt == 1:
                        dve.wait_ge(gexp_done, st.at(lambda s: a_count(s)))
                        if layer_of(s - 3) == 0:
                            link(nc.vector.reciprocal(g1[:, 0:1], gse[:, :]))
                            link(nc.vector.tensor_scalar(gp[:, :], ge[:, :], g1[:, 0:1], None, ALU.mult))
                        else:
                            link(nc.vector.tensor_scalar(g1[:, :], ge[:, :], 1.0, None, ALU.add))
                            link(nc.vector.reciprocal(g2[:, :], g1[:, :]))
                            link(nc.vector.tensor_scalar(gp[:, :], g2[:, :], bc[0:T, RS:RS + 1], None, ALU.mult))
                    if kt == 2:
                        nc.vector.tensor_tensor(ggt[:, :, :], pj, pe_, ALU.is_gt)
                        link(nc.vector.tensor_tensor(geq[:, :, :], pj, pe_, ALU.is_equal))
                        link(nc.vector.tensor_tensor(gel[:, :, :], geq[:, :, :], before_me[:, :, :], ALU.mult))
                    if kt == 3:
                        link(nc.vector.tensor_tensor(grk[:, :, :], gel[:, :, :], ggt[:, :, :], ALU.add))
                        link(nc.vector.tensor_reduce(rank[:, :], grk[:, :, :], AX.X, ALU.add))
                    if kt == 4:
                        link(nc.vector.scalar_tensor_tensor(out=gsp[:, :], in0=rank[:, :], scalar=1.5, in1=gp[:, :],
                                                            op0=ALU.is_lt, op1=ALU.mult))
                        link(nc.vector.tensor_reduce(gden[:, :], gsp[:, :], AX.X, ALU.add))
                    if kt == 5:
                        link(nc.vector.reciprocal(grd[:, :], gden[:, :]))
                        nc.vector.tensor_scalar(gate[:, 0:NE], gsp[:, :], grd[:, :], None, ALU.mult).then_inc(gate_done, 1)

                if s == 0:
                    nc.vector.memset(Vf[:, :, PR + 1:32], 0.0).then_inc(init_v, 1)
                if s == 3:
                    dve.wait_ge(f_in, 16 * 5)
                for kt in range(KT):
                    if s == 2 and kt == 2:
                        late_constants()
                    if kt == 0 and has_m(s - 1):
                        dve.wait_ge(max_done, st.at(lambda s: NMAX * s))
                        link(nc.vector.tensor_reduce(m8[:, :], mx[:, (s - 1) % 2, :, :].rearrange("t c p -> t p c"), AX.X, ALU.max))
                        if s > 1:
                            dve.wait_ge(fy_ready, st.at(lambda s: upto(fy_uses, s - 1, "ct")))
                        link(nc.vector.tensor_scalar(cc[:, 0, :], m8[:, :], 1.0 / BIG, None, ALU.mult))
                        nc.vector.scalar_tensor_tensor(out=cc[:, 1, :], in0=cc[:, 0, :], scalar=-BIG, in1=m8[:, :],
                                                       op0=ALU.mult, op1=ALU.add).then_inc(cc_ready, 1)
                    for back, use in issued_before(fy_uses, s, kt):
                        from_fy(back, use)
                    for back, use in issued_before(fh_uses, s, kt):
                        from_fh(back, use)
                    if kt == AV_LAG and is_batch(s - 2):
                        dve.wait_ge(av_done, st.at(lambda s: KT * (s - 1)))
                        if s >= 4:
                            dve.wait_ge(on_done, st.at(lambda s: s - 3))
                        nc.vector.tensor_tensor(OM[:, s % 2, :], pO[:, 0:2 * T],
                                                headmask[:, :, :, :].rearrange("p r j q -> p (r j q)"),
                                                ALU.mult).then_inc(o_free, 1)
                    if has_m(s):
                        m = MAXES_PER_KT * kt
                        dve.wait_ge(mx_ready, st.at(lambda s: NMAX * s + m + 1))
                        nc.vector.tensor_reduce(mx[:, s % 2, m // PAIRS, m % PAIRS:m % PAIRS + 1],
                                                pMX[0:T, 0, 0:CW], AX.X, ALU.max).then_inc(max_done, 1)
                    if has_a(s) and kt == 9:
                        dve.wait_ge(rstdf_done, st.at(lambda s: a_count(s) + 1))
                        nc.vector.tensor_scalar(xnf[:, :], XF[:, :], mvf[:, 0:1], rsf[:, :],
                                                ALU.subtract, ALU.mult).then_inc(xnf_done, 1)
                    if has_m(s):
                        m = MAXES_PER_KT * kt + 1
                        dve.wait_ge(mx_ready, st.at(lambda s: NMAX * s + m + 1))
                        nc.vector.tensor_reduce(mx[:, s % 2, m // PAIRS, m % PAIRS:m % PAIRS + 1],
                                                pMX[0:T, 1, 0:CW], AX.X, ALU.max).then_inc(max_done, 1)
                    if has_f(s):
                        shares(kt)
                    if has_q(s) and kt == 1:
                        if s + 1 >= B:
                            dve.wait_ge(x_done, st.at(lambda s: (s + 1 - B) // 2 + 1))
                        link(nc.vector.bn_stats(stq[:, :], xg(lambda s: (s + 1) // 2)), alone=True)
                        nc.vector.bn_aggr(mvq[:, :], stq[:, :]).then_inc(statq_done, 1)
                    if has_q(s) and s + 1 >= B and kt == 2:
                        dve.wait_ge(masksum_done, st.at(lambda s: mask_count(s) + 1))
                        nc.vector.tensor_scalar(keep[:, :], masksum[:, :], -BIG * (S2 - 0.5), None, ALU.is_gt
                                                ).then_inc(keep_done, 1)
                    if has_q(s) and kt == 3:
                        dve.wait_ge(rstdq_done, st.at(lambda s: q_count(s) + 1))
                        nc.vector.tensor_scalar(xnq[:, :], xg(lambda s: (s + 1) // 2), mvq[:, 0:1], rkq[:, :],
                                                ALU.subtract, ALU.mult).then_inc(xnq_done, 1)
                assert linked[0] == links(s), (s, linked[0], links(s))

            run_steps(dve, step)

        @block.tensor
        def _(pe):
            pe.wait_ge(init_v, 7)
            pe.wait_ge(init_p, 15)

            def score_half(st, kt, h):
                back, tile = tile_at(kt, E_LAG)
                if not is_batch(st.s - back):
                    return
                b = (st.s - back) % 2
                if tile == 0 and h == 0:
                    pe.wait_ge(qexp_in[b], st.at(lambda s: 16 * ((s - back) // 2 + 1)))
                    pe.wait_ge(shift_in, st.at(lambda s: 16 * (s - back + 1)))
                if st.s > back or tile > 0:
                    pe.wait_ge(exp_done, st.at(lambda s: 2 * (KT * (s - back) + tile) + h - 1))
                for i in range(4):
                    p = 4 * h + i
                    mm = nc.tensor.matmul(pST[0:KP, h, i * T:(i + 1) * T],
                                          kop[0:ROWS, b, p, tile * KP:(tile + 1) * KP],
                                          qexp[0:ROWS, b, p, :, :].rearrange("r j q -> r (j q)"),
                                          start=True, stop=True)
                mm.then_inc(st_ready, 1)

            def weigh(st, kt):
                back, tile = tile_at(kt, AV_LAG)
                if not is_batch(st.s - back):
                    return
                b = (st.s - back) % 2
                if tile == 0:
                    pe.wait_ge(kv_free, st.at(lambda s: upto(kv_uses, s - back, "v2", True)))
                    if st.s > back:
                        pe.wait_ge(o_free, st.at(lambda s: s - back))
                for r in range(2):
                    pe.wait_ge(exp_done, st.at(lambda s: 2 * (KT * (s - back) + tile) + r + 1))
                    for g in range(4):
                        p = 4 * r + g
                        mm = nc.tensor.matmul(pO[32 * g:32 * (g + 1), r * T:(r + 1) * T],
                                              V[0:KP, b, tile, p, :], P[0:KP, tile % RING, p * T:(p + 1) * T],
                                              start=(tile == 0 and r == 0), stop=(tile == KT - 1), skip_group_check=True)
                mm.then_inc(av_done, 1)

            def max_scores(st, m):
                c, p = divmod(m, PAIRS)
                if m == 0:
                    pe.wait_ge(qmax_in, st.at(lambda s: 96 * (s + 1)))
                    if st.s == 0:
                        pe.wait_ge(init_dma, 128)
                if p == 0:
                    pe.wait_ge(kop_in[c], st.at(b_total))
                if st.s > 0 or m > 1:
                    pe.wait_ge(max_done, st.at(lambda s: NMAX * s + m - 1))
                nc.tensor.matmul(pMX[0:T, m % 2, 0:CW],
                                 qmax[0:SHIFT0, st.s % 2, p, :, :].rearrange("r j q -> r (j q)"),
                                 kop[0:SHIFT0, st.s % 2, p, c * CW:(c + 1) * CW], start=True, stop=True
                                 ).then_inc(mx_ready, 1)

            def step(st):
                s = st.s
                if s == 3:
                    pe.wait_ge(init_l, 17)
                    pe.wait_ge(f_in, 16 * 5)
                if s == 4:
                    pe.wait_ge(f2_in, 16 * 3)

                def free(sem_, uses, name):
                    first = before(uses, s) == 0 and uses(s)[0][1] == name
                    if not first:
                        def n(s):
                            u = [x for x in uses(s) if x[1] == name][0]
                            return upto(uses, s, name, True) - u[2]
                        pe.wait_ge(sem_, st.at(n))

                for kt in range(KT):
                    late = kt in (1, 7)
                    if has_m(s) and not late:
                        max_scores(st, MAXES_PER_KT * kt)
                    if kt != AV_LAG:
                        weigh(st, kt)
                    score_half(st, kt, 0)
                    if has_m(s) and late:
                        max_scores(st, MAXES_PER_KT * kt)
                    for use in [u[1] for u in kv_uses(s) if u[0] == kt]:
                        c = int(use[1])
                        free(kv_free, kv_uses, use)
                        if use[0] == "k":
                            if s == -1:
                                pe.wait_ge(init_c, 2 * LAYERS + c + 1)
                            else:
                                pe.wait_ge(ctx_split, st.at(lambda s: CH * s + c + 1))
                            b, l, cols = (s + 1) % 2, layer_of(s + 1), slice(c * CW, (c + 1) * CW)
                            for i, (m, x_) in enumerate(((Whi, Chi), (Whi, Clo), (Wlo, Chi))):
                                mm = nc.tensor.matmul(pKV[:, 0:CW], m[:, l, 0, :], x_[:, b, cols],
                                                      start=(i == 0), stop=(i == 2))
                        else:
                            l = layer_of(s)
                            for i in range(KPC):
                                cols = slice((KPC * c + i) * KP, (KPC * c + i + 1) * KP)
                                for k, (x_, m) in enumerate(((Chi, Whi), (Chi, Wlo), (Clo, Whi))):
                                    mm = nc.tensor.matmul(pKV[0:KP, i * D:(i + 1) * D], x_[:, s % 2, cols], m[:, l, 1, :],
                                                          start=(k == 0), stop=(k == 2))
                        mm.then_inc(kv_ready, 1)
                    if has_m(s):
                        max_scores(st, MAXES_PER_KT * kt + 1)
                    score_half(st, kt, 1)

                    for use in [u[1] for u in fy_uses(s) if u[0] == kt]:
                        free(fy_free, fy_uses, use)
                        if use == "sum":
                            pe.wait_ge(o_free, st.at(lambda s: s - 1))
                            mm = nc.tensor.matmul(pFY[:, 0:2 * T], sel[:, :], OM[:, s % 2, :], start=True, stop=True)
                        elif use == "y":
                            pe.wait_ge(on_done, st.at(lambda s: s - 1))
                            l = layer_of(s - 2)
                            for r in range(2):
                                for j in range(2):
                                    mm = nc.tensor.matmul(pFY[0:T, 0:D], ON[:, r, j, :, :].rearrange("p b q -> p (b q)"), woE[:, l, r, :],
                                                          start=(r == 0 and j == 0), stop=(r == 1 and j == 1))
                        elif use == "xT":
                            pe.wait_ge(xnf_done, st.at(lambda s: a_count(s) + 1))
                            mm = nc.tensor.transpose(pFY[:, 0:T], xnf[:, :], ident[0:T, 0:T])
                        elif use == "lg":
                            mm = nc.tensor.matmul(pFY[0:T, 0:NE], xnfT[:, :], w(f"gate{layer_of(s - 2)}"),
                                                  start=True, stop=True)
                        elif use == "gT":
                            pe.wait_ge(gate_done, st.at(lambda s: f_count(s) + 1))
                            mm = nc.tensor.transpose(pFY[0:NE + 1, 0:T], gate[:, :], ident[0:T, 0:T])
                        elif use == "ct":
                            pe.wait_ge(cc_ready, st.at(lambda s: s))
                            mm = nc.tensor.transpose(pFY[0:2 * PAIRS, 0:T // 2].bitcast(F16),
                                                     cc[:, :, :].rearrange("t i p -> t (i p)"), ident16[0:T, 0:T])
                        elif use == "yb":
                            l = layer_of(s - 4)
                            if l == 1:
                                nc.tensor.matmul(pFY[0:T, 0:D], HR[0:F1, 4, :], ws2b[:, :], start=True, stop=False)
                            mm = nc.tensor.matmul(pFY[0:T, 0:D], gateT[:, :], b2x[:, l, :], start=(l == 0), stop=True)
                        else:
                            if use == "y0":
                                if s == 4:
                                    pe.wait_ge(f3_in, 32)
                                pe.wait_ge(gelu_done, st.at(lambda s: 2 * (f_count(s) + 1)))
                            l = layer_of(s - 4 if s % 2 else s - 3)
                            i = int(use[1])
                            for j, e in enumerate(experts_of(i)):
                                o = pFY[0:T, j * D:(j + 1) * D]
                                if l == 0:
                                    for c in range(F0C):
                                        mm = nc.tensor.matmul(o, HR[:, F0C * e + c, :], w2a[:, e, c, :],
                                                              start=(c == 0), stop=(c == F0C - 1))
                                else:
                                    half = slice(F1 * (e % 2), F1 * (e % 2 + 1))
                                    mm = nc.tensor.matmul(o, HR[half, e // 2, :], w2b[half, e // 2, :],
                                                          start=True, stop=True)
                        mm.then_inc(fy_ready, 1)

                    if kt == AV_LAG:
                        weigh(st, kt)
                    for use in [u[1] for u in fh_uses(s) if u[0] == kt]:
                        free(fh_free, fh_uses, use)
                        if use == "qT":
                            pe.wait_ge(xnq_done, st.at(lambda s: q_count(s) + 1))
                            nc.tensor.transpose(pFH[:, 0:T], xnq[:, :], ident[0:T, 0:T])
                            nc.tensor.transpose(pFH[0:1, 128:128 + T], keep[:, :], ident[0:T, 0:T]).then_inc(fh_ready, 1)
                        elif use == "q":
                            l = layer_of(s + 1)
                            nc.tensor.matmul(pFH[:, 0:T], w(f"wq{l}"), xnqT[:, :], start=True, stop=False)
                            nc.tensor.matmul(pFH[:, 0:T], bq_row[:, l * D:(l + 1) * D], keepT[:, :],
                                             start=False, stop=True).then_inc(fh_ready, 1)
                        else:
                            e = int(use[1:])
                            l = layer_of(s - 2 if s % 2 else s - 3)
                            if l == 0:
                                for c in range(F0C):
                                    mm = nc.tensor.matmul(pFH[:, c * T:(c + 1) * T], w1a[:, e, c * 128:(c + 1) * 128],
                                                          xnfT[:, :], start=True, stop=True)
                            elif e == 0:
                                for c in range(4):
                                    mm = nc.tensor.matmul(
                                        pFH[:, c * T:(c + 1) * T],
                                        w1b[:, 2 * c:2 * c + 2, :].rearrange("d e f -> d (e f)"),
                                        xnfT[:, :], start=True, stop=True)
                            else:
                                mm = nc.tensor.matmul(pFH[0:F1, 0:T], w("ws1"), xnfT[:, :], start=True, stop=True)
                            mm.then_inc(fh_ready, 1)

            run_steps(pe, step)


def kernel(**inputs):
    import numpy as np
    import concourse.bacc as bacc
    from concourse.bass_utils import run_bass_kernel_spmd

    def arr(name):
        return np.asarray(inputs[name])

    def pairs_last(a):
        return a.reshape(a.shape[:-1] + (PAIRS, PR)).swapaxes(-1, -2).reshape(a.shape)

    x0 = arr("x")
    wq = [arr("L0_xattn_Wq").T, arr("L1_xattn_wq_kernel")]
    wk = [arr("L0_xattn_Wk").T, arr("L1_xattn_wk_kernel")]
    wv = [arr("L0_xattn_Wv").T, arr("L1_xattn_wv_kernel")]
    parts = {"bk0": pairs_last(arr("L0_xattn_bk"))[:, None], "bk1": pairs_last(arr("L1_xattn_wk_bias"))[:, None],
             "gate0": arr("L0_ffn_gate_w"), "gate1": arr("L1_ffn_gate_W"),
             "b1_0": arr("L0_ffn_b1").reshape(E0 * F0C, 128).T, "b1_1": arr("L1_ffn_b1").reshape(-1, 128).T,
             "ws1": arr("L1_ffn_Ws1")}
    for l in range(LAYERS):
        parts[f"wq{l}"], parts[f"wk{l}"], parts[f"wv{l}"] = pairs_last(wq[l]), pairs_last(wk[l]), wv[l]
    arrays = {
        "x": x0.reshape(B * S, D),
        "ctxT": arr("ctx_1024").transpose(0, 2, 1),
        "mask": arr("mask_BxSxS2_ik1").reshape(G, T, S2),
        "wpack": np.concatenate([parts[n] for n in COLS], axis=1),
        "bqrow": np.concatenate([pairs_last(arr("L0_xattn_bq")), pairs_last(arr("L1_xattn_wq_bias"))])[None],
        "bcast": np.concatenate([arr("L0_xattn_bo"), arr("L1_xattn_wo_bias"), arr("g_xattn"), arr("g_ffn"),
                                 arr("L1_ffn_route_scale").reshape(1)]),
        "wo": np.stack([arr("L0_xattn_Wo").T, arr("L1_xattn_wo_kernel")]),
        "bvc": np.stack([arr("L0_xattn_bv"), arr("L1_xattn_wv_bias")]).reshape(LAYERS, 2, 4, PR).transpose(0, 2, 3, 1),
        "w1_0": arr("L0_ffn_w1"), "w2_0": arr("L0_ffn_w2"), "b2_0": arr("L0_ffn_b2"),
        "w1_1": arr("L1_ffn_W1"), "w2_1": arr("L1_ffn_W2"),
        "b2_1": np.concatenate([arr("L1_ffn_b2"), arr("L1_ffn_bs2")[None]]),
        "ws2": arr("L1_ffn_Ws2"), "bs1": arr("L1_ffn_bs1")[:, None],
    }
    nc = bacc.Bacc("TRN2", target_bir_lowering=False, num_devices=1)
    given, args = {}, []
    for name, a in arrays.items():
        a = np.ascontiguousarray(a)
        given[f"in_{name}"] = a
        args.append(nc.dram_tensor(f"in_{name}", a.shape, mybir.dt.from_np(a.dtype), kind="ExternalInput").ap())
    args.append(nc.dram_tensor("out_0", (B * S, D), F32, kind="ExternalOutput").ap())
    build(nc, *args)
    r = run_bass_kernel_spmd(nc, [given], core_ids=[0])
    return r.results[0]["out_0"].reshape(B, S, D)
```
